# Optimizing a Trainium2 kernel written in Bass

```python
import numpy as np
import jax
import jax.numpy as jnp

def _softmax(x, axis=-1):
    return jax.nn.softmax(x, axis=axis)

def _gelu(x):
    return jax.nn.gelu(x, approximate=True)

def _silu(x):
    return jax.nn.silu(x)

def _sigmoid(x):
    return jax.nn.sigmoid(x)

def _layernorm(x, axis=-1, eps=1e-05):
    m = jnp.mean(x, axis=axis, keepdims=True)
    v = jnp.var(x, axis=axis, keepdims=True)
    return (x - m) / jnp.sqrt(v + eps)

def _scatter_add(tgt, idx, src, axis=0):
    return tgt.at[idx].add(src)

def _segment_sum(src, seg, n):
    return jax.ops.segment_sum(src, seg, n)
kernel_name = 'mk_vit_tower_d2_tok_img768_r4_db6919'

def setup_inputs(seed: int=0):
    np.random.seed(seed)
    _w = jnp.asarray

    def _rec_inputs():
        import jax
        import jax.numpy as jnp
        _rk = jax.random.key(seed)
        x = -0.000356955 + 1 * jax.random.normal(jax.random.fold_in(_rk, 1), (64, 3, 112, 112), jnp.float32)
        return x
    x = _rec_inputs()

    def _L0_tok_setup():
        import jax, jax.numpy as jnp
        import numpy as np
        PATCH = 16
        EMB = 192
        key = jax.random.key(seed)
        k1, k2 = jax.random.split(key)
        x = jax.random.normal(k1, (128, 3, 224, 224), dtype=jnp.float32)
        W = jax.random.normal(k2, (EMB, PATCH * PATCH * 3), dtype=jnp.float32) * 0.02
        return {'x': x, 'W': W}
    _L0_tok_all = _L0_tok_setup()
    _L0_tok_in = {k: v for k, v in _L0_tok_all.items() if k in ('W',)}
    del _L0_tok_all

    def _L0_attn_setup():
        import jax, jax.numpy as jnp
        import numpy as np
        D_MODEL = 192
        D_STATE = 16
        D_CONV = 4
        EXPAND = 2
        D_INNER = EXPAND * D_MODEL
        DT_RANK = (D_MODEL + 15) // 16
        BATCH = 2
        SEQLEN = 256

        def _mamba(x, in_w, conv_w, conv_b, xproj_w, dt_w, dt_b, A_log, Dp, out_w):
            B, L, _ = x.shape
            xz = x @ in_w.T
            xc, z = jnp.split(xz, 2, axis=-1)
            K = conv_w.shape[1]
            xpad = jnp.pad(xc, ((0, 0), (K - 1, 0), (0, 0)))
            xconv = conv_b + sum((conv_w[:, k] * xpad[:, k:k + L, :] for k in range(K)))
            u = jax.nn.silu(xconv)
            proj = u @ xproj_w.T
            dt_rank = dt_w.shape[1]
            n = A_log.shape[1]
            dtx, Bm, Cm = jnp.split(proj, [dt_rank, dt_rank + n], axis=-1)
            dt = jax.nn.softplus(dtx @ dt_w.T + dt_b)
            A = -jnp.exp(A_log)
            dA = jnp.exp(dt[..., None] * A)
            dBu = dt[..., None] * Bm[:, :, None, :] * u[..., None]

            def step(h, inp):
                dA_t, dBu_t, C_t = inp
                h = dA_t * h + dBu_t
                y = jnp.einsum('bdn,bn->bd', h, C_t)
                return (h, y)
            h0 = jnp.zeros((B, u.shape[-1], n), x.dtype)
            _, ys = jax.lax.scan(step, h0, (dA.transpose(1, 0, 2, 3), dBu.transpose(1, 0, 2, 3), Cm.transpose(1, 0, 2)))
            y = ys.transpose(1, 0, 2) + u * Dp
            y = y * jax.nn.silu(z)
            return y @ out_w.T
        key = jax.random.key(seed)
        ks = jax.random.split(key, 10)
        s = 0.02
        f32 = jnp.float32
        x = jax.random.normal(ks[0], (BATCH, SEQLEN, D_MODEL), f32)
        bm_in_w = jax.random.normal(ks[1], (2 * D_MODEL, D_MODEL), f32) * s
        bm_in_b = jnp.zeros((2 * D_MODEL,), f32)
        bm_out_w = jax.random.normal(ks[2], (D_MODEL, D_MODEL), f32) * s
        bm_out_b = jnp.zeros((D_MODEL,), f32)
        m_in_w = jax.random.normal(ks[3], (2 * D_INNER, D_MODEL), f32) * s
        m_conv_w = jax.random.normal(ks[4], (D_INNER, D_CONV), f32) * s
        m_conv_b = jnp.zeros((D_INNER,), f32)
        m_xproj_w = jax.random.normal(ks[5], (DT_RANK + 2 * D_STATE, D_INNER), f32) * s
        m_dt_w = jax.random.normal(ks[6], (D_INNER, DT_RANK), f32) * s
        m_dt_b = jnp.full((D_INNER,), -4.6, f32)
        m_A_log = jnp.log(jnp.broadcast_to(jnp.arange(1, D_STATE + 1, dtype=f32), (D_INNER, D_STATE)))
        m_D = jnp.ones((D_INNER,), f32)
        m_out_w = jax.random.normal(ks[7], (D_MODEL, D_INNER), f32) * s
        ln_g = jnp.ones((D_MODEL,), f32)
        ln_b = jnp.zeros((D_MODEL,), f32)
        return {'x': x, 'bm_in_w': bm_in_w, 'bm_in_b': bm_in_b, 'bm_out_w': bm_out_w, 'bm_out_b': bm_out_b, 'm_in_w': m_in_w, 'm_conv_w': m_conv_w, 'm_conv_b': m_conv_b, 'm_xproj_w': m_xproj_w, 'm_dt_w': m_dt_w, 'm_dt_b': m_dt_b, 'm_A_log': m_A_log, 'm_D': m_D, 'm_out_w': m_out_w, 'ln_g': ln_g, 'ln_b': ln_b}
    _L0_attn_all = _L0_attn_setup()
    _L0_attn_in = {k: v for k, v in _L0_attn_all.items() if k in ('bm_in_w', 'bm_in_b', 'bm_out_w', 'bm_out_b', 'm_in_w', 'm_conv_w', 'm_conv_b', 'm_xproj_w', 'm_dt_w', 'm_dt_b', 'm_A_log', 'm_D', 'm_out_w', 'ln_g', 'ln_b')}
    del _L0_attn_all

    def _L0_ffn_setup():
        import jax, jax.numpy as jnp
        import numpy as np
        B, T, C = (2, 256, 192)
        H, NE, K = (768, 8, 2)
        key = jax.random.key(seed)
        k1, k2, k3, k4 = jax.random.split(key, 4)
        x = jax.random.normal(k1, (B, T, C), dtype=jnp.float32)
        w_fc = jax.random.normal(k2, (C, H * NE), dtype=jnp.float32) * 0.02
        w_proj = jax.random.normal(k3, (H * NE, C), dtype=jnp.float32) * (0.02 * (2 * 12) ** (-0.5))
        w_gate = jax.random.normal(k4, (C, NE), dtype=jnp.float32) * 0.02
        return {'x': x, 'w_fc': w_fc, 'w_proj': w_proj, 'w_gate': w_gate}
    _L0_ffn_all = _L0_ffn_setup()
    _L0_ffn_in = {k: v for k, v in _L0_ffn_all.items() if k in ('w_fc', 'w_proj', 'w_gate')}
    del _L0_ffn_all

    def _L1_attn_setup():
        import jax, jax.numpy as jnp
        import numpy as np
        from jax import lax
        H = 192
        I = 384
        N = 16
        R = 48
        K = 4
        NL = 16
        B, L = (2, 256)
        EPS = 1e-05

        def rmsnorm(x, w):
            return x * lax.rsqrt(jnp.mean(x * x, axis=-1, keepdims=True) + EPS) * w

        def causal_conv(u, w, b):
            uc = jnp.swapaxes(u, 1, 2)
            y = lax.conv_general_dilated(uc, w, (1,), [(K - 1, 0)], dimension_numbers=('NCH', 'OIH', 'NCH'), feature_group_count=I)
            return jnp.swapaxes(y + b[None, :, None], 1, 2)

        def selective_scan(u, dt, A, Bm, Cm, Dp):

            def step(h, inp):
                u_t, dt_t, B_t, C_t = inp
                dA = jnp.exp(dt_t[:, :, None] * A)
                h = dA * h + (dt_t * u_t)[:, :, None] * B_t[:, None, :]
                y = jnp.einsum('bin,bn->bi', h, C_t)
                return (h, y)
            inputs = tuple((jnp.moveaxis(a, 1, 0) for a in (u, dt, Bm, Cm)))
            h0 = jnp.zeros((u.shape[0],) + A.shape, u.dtype)
            _, ys = lax.scan(step, h0, inputs)
            return jnp.moveaxis(ys, 0, 1) + u * Dp

        def mamba_layer(x, p):
            in_w, cw, cb, xp_w, dtw, dtb, a_log, dp, ow, nw = p
            h = rmsnorm(x, nw)
            xz = jnp.einsum('blh,ch->blc', h, in_w)
            u, z = jnp.split(xz, 2, axis=-1)
            u = jax.nn.silu(causal_conv(u, cw, cb))
            proj = jnp.einsum('bli,ci->blc', u, xp_w)
            dt_r, Bm, Cm = (proj[..., :R], proj[..., R:R + N], proj[..., R + N:])
            dt = jax.nn.softplus(jnp.einsum('blr,ir->bli', dt_r, dtw) + dtb)
            A = -jnp.exp(a_log)
            y = selective_scan(u, dt, A, Bm, Cm, dp)
            y = y * jax.nn.silu(z)
            return x + jnp.einsum('bli,hi->blh', y, ow)
        key = jax.random.key(seed)
        ks = jax.random.split(key, 8)
        s = 0.02
        x = jax.random.normal(ks[0], (B, L, H), jnp.float32)
        in_proj_w = jax.random.normal(ks[1], (NL, 2 * I, H), jnp.float32) * s
        conv_w = jax.random.normal(ks[2], (NL, I, 1, K), jnp.float32) * 0.1
        conv_b = jnp.zeros((NL, I), jnp.float32)
        x_proj_w = jax.random.normal(ks[3], (NL, R + 2 * N, I), jnp.float32) * s
        dt_proj_w = jax.random.normal(ks[4], (NL, I, R), jnp.float32) * 0.01
        dt_proj_b = -4.0 + 0.1 * jax.random.normal(ks[5], (NL, I), jnp.float32)
        A_log = jnp.log(jnp.tile(jnp.arange(1, N + 1, dtype=jnp.float32), (NL, I, 1)))
        D = jnp.ones((NL, I), jnp.float32)
        out_proj_w = jax.random.normal(ks[6], (NL, H, I), jnp.float32) * s
        norm_w = jnp.ones((NL, H), jnp.float32)
        final_norm_w = jnp.ones((H,), jnp.float32)
        return {'x': x, 'in_proj_w': in_proj_w, 'conv_w': conv_w, 'conv_b': conv_b, 'x_proj_w': x_proj_w, 'dt_proj_w': dt_proj_w, 'dt_proj_b': dt_proj_b, 'A_log': A_log, 'D': D, 'out_proj_w': out_proj_w, 'norm_w': norm_w, 'final_norm_w': final_norm_w}
    _L1_attn_all = _L1_attn_setup()
    _L1_attn_in = {k: v for k, v in _L1_attn_all.items() if k in ('in_proj_w', 'conv_w', 'conv_b', 'x_proj_w', 'dt_proj_w', 'dt_proj_b', 'A_log', 'D', 'out_proj_w', 'norm_w', 'final_norm_w')}
    del _L1_attn_all

    def _L1_ffn_setup():
        import jax, jax.numpy as jnp
        import numpy as np
        LN2 = jnp.log(jnp.float32(2.0))
        ALPHA = 0.5
        A_BITS = 8
        W_BITS = 8
        EPS = 1e-08

        def round_ln(x):
            y = jnp.floor(jnp.log(x) / LN2)
            up = x - 2.0 ** y > 2.0 ** (y + 1.0) - x
            return y + up.astype(x.dtype)

        def fq_act_asym(x, bits=A_BITS):
            qmax = 2 ** bits - 1
            xmin = jnp.minimum(x.min(), 0.0)
            xmax = jnp.maximum(x.max(), 0.0)
            scale = jnp.maximum((xmax - xmin) / qmax, EPS)
            zp = jnp.round(-xmin / scale)
            q = jnp.clip(jnp.round(x / scale) + zp, 0, qmax)
            return (q - zp) * scale

        def fq_act_sym(x, bits=A_BITS):
            qmax = 2 ** (bits - 1) - 1
            scale = jnp.maximum(jnp.abs(x).max() / qmax, EPS)
            q = jnp.clip(jnp.round(x / scale), -qmax - 1, qmax)
            return q * scale

        def fq_weight(w, bits=W_BITS):
            qmax = 2 ** (bits - 1) - 1
            scale = jnp.maximum(jnp.abs(w).max(axis=1, keepdims=True) / qmax, EPS)
            q = jnp.clip(jnp.round(w / scale), -qmax - 1, qmax)
            return q * scale
        key = jax.random.key(seed)
        ks = jax.random.split(key, 5)
        B, N, C, H = (64, 197, 192, 768)
        x = jax.random.normal(ks[0], (B, N, C), dtype=jnp.float32)
        w1 = jax.random.normal(ks[1], (H, C), dtype=jnp.float32) * 0.02
        b1 = jax.random.normal(ks[2], (H,), dtype=jnp.float32) * 0.02
        w2 = jax.random.normal(ks[3], (C, H), dtype=jnp.float32) * 0.02
        b2 = jax.random.normal(ks[4], (C,), dtype=jnp.float32) * 0.02
        return {'x': x, 'w1': w1, 'b1': b1, 'w2': w2, 'b2': b2}
    _L1_ffn_all = _L1_ffn_setup()
    _L1_ffn_in = {k: v for k, v in _L1_ffn_all.items() if k in ('w1', 'b1', 'w2', 'b2')}
    del _L1_ffn_all
    return {'x': x, 'L0_tok_W': _L0_tok_in['W'], 'L0_attn_bm_in_w': _L0_attn_in['bm_in_w'], 'L0_attn_bm_in_b': _L0_attn_in['bm_in_b'], 'L0_attn_bm_out_w': _L0_attn_in['bm_out_w'], 'L0_attn_bm_out_b': _L0_attn_in['bm_out_b'], 'L0_attn_m_in_w': _L0_attn_in['m_in_w'], 'L0_attn_m_conv_w': _L0_attn_in['m_conv_w'], 'L0_attn_m_conv_b': _L0_attn_in['m_conv_b'], 'L0_attn_m_xproj_w': _L0_attn_in['m_xproj_w'], 'L0_attn_m_dt_w': _L0_attn_in['m_dt_w'], 'L0_attn_m_dt_b': _L0_attn_in['m_dt_b'], 'L0_attn_m_A_log': _L0_attn_in['m_A_log'], 'L0_attn_m_D': _L0_attn_in['m_D'], 'L0_attn_m_out_w': _L0_attn_in['m_out_w'], 'L0_attn_ln_g': _L0_attn_in['ln_g'], 'L0_attn_ln_b': _L0_attn_in['ln_b'], 'L0_ffn_w_fc': _L0_ffn_in['w_fc'], 'L0_ffn_w_proj': _L0_ffn_in['w_proj'], 'L0_ffn_w_gate': _L0_ffn_in['w_gate'], 'L1_attn_in_proj_w': _L1_attn_in['in_proj_w'], 'L1_attn_conv_w': _L1_attn_in['conv_w'], 'L1_attn_conv_b': _L1_attn_in['conv_b'], 'L1_attn_x_proj_w': _L1_attn_in['x_proj_w'], 'L1_attn_dt_proj_w': _L1_attn_in['dt_proj_w'], 'L1_attn_dt_proj_b': _L1_attn_in['dt_proj_b'], 'L1_attn_A_log': _L1_attn_in['A_log'], 'L1_attn_D': _L1_attn_in['D'], 'L1_attn_out_proj_w': _L1_attn_in['out_proj_w'], 'L1_attn_norm_w': _L1_attn_in['norm_w'], 'L1_attn_final_norm_w': _L1_attn_in['final_norm_w'], 'L1_ffn_w1': _L1_ffn_in['w1'], 'L1_ffn_b1': _L1_ffn_in['b1'], 'L1_ffn_w2': _L1_ffn_in['w2'], 'L1_ffn_b2': _L1_ffn_in['b2']}

def reference(x, L0_tok_W, L0_attn_bm_in_w, L0_attn_bm_in_b, L0_attn_bm_out_w, L0_attn_bm_out_b, L0_attn_m_in_w, L0_attn_m_conv_w, L0_attn_m_conv_b, L0_attn_m_xproj_w, L0_attn_m_dt_w, L0_attn_m_dt_b, L0_attn_m_A_log, L0_attn_m_D, L0_attn_m_out_w, L0_attn_ln_g, L0_attn_ln_b, L0_ffn_w_fc, L0_ffn_w_proj, L0_ffn_w_gate, L1_attn_in_proj_w, L1_attn_conv_w, L1_attn_conv_b, L1_attn_x_proj_w, L1_attn_dt_proj_w, L1_attn_dt_proj_b, L1_attn_A_log, L1_attn_D, L1_attn_out_proj_w, L1_attn_norm_w, L1_attn_final_norm_w, L1_ffn_w1, L1_ffn_b1, L1_ffn_w2, L1_ffn_b2):
    import jax
    import jax.numpy as jnp

    def _L0_tok_ref(x, W):
        import jax, jax.numpy as jnp
        import numpy as np
        PATCH = 16
        EMB = 192
        B, C, H, Wd = x.shape
        p = PATCH
        hp, wp = (H // p, Wd // p)
        num_patches = hp * wp
        xp = x.reshape(B, C, hp, p, wp, p).transpose(0, 1, 2, 4, 3, 5)
        xp = xp.reshape(B, C, num_patches, p, p).transpose(0, 2, 1, 3, 4)
        xp = xp.reshape(B, num_patches, C * p * p)
        return jnp.einsum('bnf,ef->bne', xp, W)

    def _L0_attn_ref(x, bm_in_w, bm_in_b, bm_out_w, bm_out_b, m_in_w, m_conv_w, m_conv_b, m_xproj_w, m_dt_w, m_dt_b, m_A_log, m_D, m_out_w, ln_g, ln_b):
        import jax, jax.numpy as jnp
        import numpy as np
        D_MODEL = 192
        D_STATE = 16
        D_CONV = 4
        EXPAND = 2
        D_INNER = EXPAND * D_MODEL
        DT_RANK = (D_MODEL + 15) // 16
        BATCH = 2
        SEQLEN = 256

        def _mamba(x, in_w, conv_w, conv_b, xproj_w, dt_w, dt_b, A_log, Dp, out_w):
            B, L, _ = x.shape
            xz = x @ in_w.T
            xc, z = jnp.split(xz, 2, axis=-1)
            K = conv_w.shape[1]
            xpad = jnp.pad(xc, ((0, 0), (K - 1, 0), (0, 0)))
            xconv = conv_b + sum((conv_w[:, k] * xpad[:, k:k + L, :] for k in range(K)))
            u = jax.nn.silu(xconv)
            proj = u @ xproj_w.T
            dt_rank = dt_w.shape[1]
            n = A_log.shape[1]
            dtx, Bm, Cm = jnp.split(proj, [dt_rank, dt_rank + n], axis=-1)
            dt = jax.nn.softplus(dtx @ dt_w.T + dt_b)
            A = -jnp.exp(A_log)
            dA = jnp.exp(dt[..., None] * A)
            dBu = dt[..., None] * Bm[:, :, None, :] * u[..., None]

            def step(h, inp):
                dA_t, dBu_t, C_t = inp
                h = dA_t * h + dBu_t
                y = jnp.einsum('bdn,bn->bd', h, C_t)
                return (h, y)
            h0 = jnp.zeros((B, u.shape[-1], n), x.dtype)
            _, ys = jax.lax.scan(step, h0, (dA.transpose(1, 0, 2, 3), dBu.transpose(1, 0, 2, 3), Cm.transpose(1, 0, 2)))
            y = ys.transpose(1, 0, 2) + u * Dp
            y = y * jax.nn.silu(z)
            return y @ out_w.T
        mparams = (m_in_w, m_conv_w, m_conv_b, m_xproj_w, m_dt_w, m_dt_b, m_A_log, m_D, m_out_w)
        xp = x @ bm_in_w.T + bm_in_b
        x_f, x_b = jnp.split(xp, 2, axis=-1)
        out_f = _mamba(x_f, *mparams)
        out_b = jnp.flip(_mamba(jnp.flip(x_b, axis=1), *mparams), axis=1)
        mo = (out_f + out_b) @ bm_out_w.T + bm_out_b
        h = mo + x
        mu = jnp.mean(h, axis=-1, keepdims=True)
        var = jnp.mean(jnp.square(h - mu), axis=-1, keepdims=True)
        return (h - mu) * jax.lax.rsqrt(var + 1e-05) * ln_g + ln_b

    def _L0_ffn_ref(x, w_fc, w_proj, w_gate):
        import jax, jax.numpy as jnp
        import numpy as np
        B, T, C = (2, 256, 192)
        H, NE, K = (768, 8, 2)
        router_logits = jnp.einsum('btc,ce->bte', x, w_gate)
        router_probs = jax.nn.softmax(router_logits, axis=-1)
        top_p, top_i = jax.lax.top_k(router_probs, K)
        top_p = top_p / jnp.sum(top_p, axis=-1, keepdims=True)
        wf = w_fc.reshape(C, H, NE)
        h_all = jnp.einsum('btc,che->bthe', x, wf)
        h = jnp.take_along_axis(h_all, top_i[:, :, None, :], axis=-1)
        h = jax.nn.gelu(h, approximate=True)
        wp = w_proj.reshape(H, C, NE)
        o_all = jnp.einsum('bthk,hce->btcke', h, wp)
        o = jnp.take_along_axis(o_all, top_i[:, :, None, :, None], axis=-1)[..., 0]
        o = jnp.einsum('btck,btk->btc', o, top_p)
        return o

    def _L1_attn_ref(x, in_proj_w, conv_w, conv_b, x_proj_w, dt_proj_w, dt_proj_b, A_log, D, out_proj_w, norm_w, final_norm_w):
        import jax, jax.numpy as jnp
        import numpy as np
        from jax import lax
        H = 192
        I = 384
        N = 16
        R = 48
        K = 4
        NL = 16
        B, L = (2, 256)
        EPS = 1e-05

        def rmsnorm(x, w):
            return x * lax.rsqrt(jnp.mean(x * x, axis=-1, keepdims=True) + EPS) * w

        def causal_conv(u, w, b):
            uc = jnp.swapaxes(u, 1, 2)
            y = lax.conv_general_dilated(uc, w, (1,), [(K - 1, 0)], dimension_numbers=('NCH', 'OIH', 'NCH'), feature_group_count=I)
            return jnp.swapaxes(y + b[None, :, None], 1, 2)

        def selective_scan(u, dt, A, Bm, Cm, Dp):

            def step(h, inp):
                u_t, dt_t, B_t, C_t = inp
                dA = jnp.exp(dt_t[:, :, None] * A)
                h = dA * h + (dt_t * u_t)[:, :, None] * B_t[:, None, :]
                y = jnp.einsum('bin,bn->bi', h, C_t)
                return (h, y)
            inputs = tuple((jnp.moveaxis(a, 1, 0) for a in (u, dt, Bm, Cm)))
            h0 = jnp.zeros((u.shape[0],) + A.shape, u.dtype)
            _, ys = lax.scan(step, h0, inputs)
            return jnp.moveaxis(ys, 0, 1) + u * Dp

        def mamba_layer(x, p):
            in_w, cw, cb, xp_w, dtw, dtb, a_log, dp, ow, nw = p
            h = rmsnorm(x, nw)
            xz = jnp.einsum('blh,ch->blc', h, in_w)
            u, z = jnp.split(xz, 2, axis=-1)
            u = jax.nn.silu(causal_conv(u, cw, cb))
            proj = jnp.einsum('bli,ci->blc', u, xp_w)
            dt_r, Bm, Cm = (proj[..., :R], proj[..., R:R + N], proj[..., R + N:])
            dt = jax.nn.softplus(jnp.einsum('blr,ir->bli', dt_r, dtw) + dtb)
            A = -jnp.exp(a_log)
            y = selective_scan(u, dt, A, Bm, Cm, dp)
            y = y * jax.nn.silu(z)
            return x + jnp.einsum('bli,hi->blh', y, ow)
        params = (in_proj_w, conv_w, conv_b, x_proj_w, dt_proj_w, dt_proj_b, A_log, D, out_proj_w, norm_w)

        def body(carry, p):
            return (mamba_layer(carry, p), None)
        out, _ = lax.scan(body, x, params)
        return rmsnorm(out, final_norm_w)

    def _L1_ffn_ref(x, w1, b1, w2, b2):
        import jax, jax.numpy as jnp
        import numpy as np
        LN2 = jnp.log(jnp.float32(2.0))
        ALPHA = 0.5
        A_BITS = 8
        W_BITS = 8
        EPS = 1e-08

        def round_ln(x):
            y = jnp.floor(jnp.log(x) / LN2)
            up = x - 2.0 ** y > 2.0 ** (y + 1.0) - x
            return y + up.astype(x.dtype)

        def fq_act_asym(x, bits=A_BITS):
            qmax = 2 ** bits - 1
            xmin = jnp.minimum(x.min(), 0.0)
            xmax = jnp.maximum(x.max(), 0.0)
            scale = jnp.maximum((xmax - xmin) / qmax, EPS)
            zp = jnp.round(-xmin / scale)
            q = jnp.clip(jnp.round(x / scale) + zp, 0, qmax)
            return (q - zp) * scale

        def fq_act_sym(x, bits=A_BITS):
            qmax = 2 ** (bits - 1) - 1
            scale = jnp.maximum(jnp.abs(x).max() / qmax, EPS)
            q = jnp.clip(jnp.round(x / scale), -qmax - 1, qmax)
            return q * scale

        def fq_weight(w, bits=W_BITS):
            qmax = 2 ** (bits - 1) - 1
            scale = jnp.maximum(jnp.abs(w).max(axis=1, keepdims=True) / qmax, EPS)
            q = jnp.clip(jnp.round(w / scale), -qmax - 1, qmax)
            return q * scale
        global_max_x = jnp.abs(x).max(axis=(0, 1))
        max_weight = jnp.abs(w1).max(axis=0)
        cs = global_max_x ** ALPHA / max_weight ** (1.0 - ALPHA)
        cs = 2.0 ** round_ln(cs)
        x_smoothed = x / cs[None, None, :]
        w1_smoothed = w1 * cs[None, :]
        xq = fq_act_asym(x_smoothed)
        h = jnp.einsum('bnc,hc->bnh', xq, fq_weight(w1_smoothed)) + b1
        h = jax.nn.gelu(h, approximate=False)
        hq = fq_act_sym(h)
        out = jnp.einsum('bnh,ch->bnc', hq, fq_weight(w2)) + b2
        out = fq_act_asym(out)
        return out
    h = _L0_tok_ref(x, L0_tok_W)
    h = h + _L0_attn_ref(_layernorm(h, axis=-1), L0_attn_bm_in_w, L0_attn_bm_in_b, L0_attn_bm_out_w, L0_attn_bm_out_b, L0_attn_m_in_w, L0_attn_m_conv_w, L0_attn_m_conv_b, L0_attn_m_xproj_w, L0_attn_m_dt_w, L0_attn_m_dt_b, L0_attn_m_A_log, L0_attn_m_D, L0_attn_m_out_w, L0_attn_ln_g, L0_attn_ln_b)
    h = h + _L0_ffn_ref(_layernorm(h, axis=-1), L0_ffn_w_fc, L0_ffn_w_proj, L0_ffn_w_gate)
    h = h + _L1_attn_ref(_layernorm(h, axis=-1), L1_attn_in_proj_w, L1_attn_conv_w, L1_attn_conv_b, L1_attn_x_proj_w, L1_attn_dt_proj_w, L1_attn_dt_proj_b, L1_attn_A_log, L1_attn_D, L1_attn_out_proj_w, L1_attn_norm_w, L1_attn_final_norm_w)
    h = h + _L1_ffn_ref(_layernorm(h, axis=-1), L1_ffn_w1, L1_ffn_b1, L1_ffn_w2, L1_ffn_b2)
    return h

_drawn_inputs = setup_inputs


def setup_inputs(seed=0):
    import zlib

    import numpy as np

    out = dict(_drawn_inputs(seed))
    spreads = {'L0_attn_bm_in_b': (0.0, 0.8),
     'L0_attn_bm_out_b': (0.0, 0.727),
     'L0_attn_m_conv_b': (0.0, 0.8),
     'L0_attn_m_dt_b': (-4.599999904632568, 0.6),
     'L0_attn_m_D': (1.0, 0.6),
     'L0_attn_ln_g': (1.0, 0.2),
     'L0_attn_ln_b': (0.0, 0.1),
     'L1_attn_conv_b': (0.0, 0.8),
     'L1_attn_D': (1.0, 0.6),
     'L1_attn_norm_w': (1.0, 0.6),
     'L1_attn_final_norm_w': (1.0, 0.2)}
    factors = {'L0_attn_bm_in_w': 8.0,
     'L0_attn_bm_out_w': 8.0,
     'L0_attn_m_in_w': 8.0,
     'L0_attn_m_conv_w': 8.0,
     'L0_attn_m_xproj_w': 8.0,
     'L0_attn_m_dt_w': 8.0,
     'L0_attn_m_A_log': 8.0,
     'L0_attn_m_out_w': 8.0,
     'L0_ffn_w_fc': 7.742,
     'L0_ffn_w_proj': 7.595,
     'L0_ffn_w_gate': 8.0,
     'L1_attn_in_proj_w': 8.0,
     'L1_attn_conv_w': 8.0,
     'L1_attn_x_proj_w': 8.0,
     'L1_attn_dt_proj_w': 8.0,
     'L1_attn_dt_proj_b': 8.0,
     'L1_attn_A_log': 8.0,
     'L1_attn_out_proj_w': 8.0,
     'L1_ffn_b1': 8.0,
     'L1_ffn_b2': 7.613}
    for name, (base, spread) in spreads.items():
        noise = np.random.default_rng([zlib.crc32(name.encode()), seed]).standard_normal(out[name].shape)
        drawn = base * np.exp(spread * noise) if base else spread * noise
        out[name] = jnp.asarray(drawn.astype(out[name].dtype))
    for name, factor in factors.items():
        out[name] = (out[name] * factor).astype(out[name].dtype)
    return out
```

```python
from contextlib import ExitStack

import concourse.bass as bass
from concourse import mybir

ALU = mybir.AluOpType
ACT = mybir.ActivationFunctionType
AX = mybir.AxisListType
F32 = mybir.dt.float32
BF16 = mybir.dt.bfloat16
I32 = mybir.dt.int32
RMAX = bass.bass_isa.ReduceOp.max

SEQS, LEN = 64, 49
T = SEQS * LEN
CHUNKS = 8
CS = SEQS // CHUNKS
CT = CS * LEN
C, HC = 192, 96
PK = 768 // 128
DT = 3
NS = 16
RANK = 48
LAYERS = 16
EXPERTS, HID = 8, 768
HT = HID // 128
BLK = 98
NBLK = T // BLK
EPS = 1e-5
EXP_SET = "natural_log_exp_and_others"
SMALL = 2.0 ** -11
LOG_SMALL = SMALL - SMALL ** 2 / 2 + SMALL ** 3 / 3
ROUND = 12582912.0

LOW = 64 + RANK
P_A, P_D, P_CW, P_CB, P_DTB, P_NW, P_END = 0, 48, 51, 63, 66, 69, 71
N_CORE = P_CW - P_A
N_PRE = P_NW - P_CW


def seqs(ap):
    return ap.rearrange("p (s t) -> p s t", t=LEN)


def chunk_of(k):
    return (k % CHUNKS) * CT


def embed(nc, const, patches, w_tok, H):
    with ExitStack() as ctx:
        w = ctx.enter_context(nc.sbuf_tensor("tok_w", [128, PK, C], F32))
        px = [ctx.enter_context(nc.sbuf_tensor(f"patches{i}", [128, PK, CT], F32)) for i in range(2)]
        acc = [ctx.enter_context(nc.psum_tensor(f"emb_ps{i}", [HC, 512], F32)) for i in range(4)]
        w_loaded = nc.alloc_semaphore("emb_w_loaded")
        px_loaded = [nc.alloc_semaphore(f"emb_px_loaded{i}") for i in range(2)]
        h_summed = nc.alloc_semaphore("emb_h_summed")
        h_copied = nc.alloc_semaphore("emb_h_copied")
        consts_loaded = nc.alloc_semaphore("consts_loaded")
        consts_set = nc.alloc_semaphore("consts_set")
        with nc.Block() as block:
            @block.sync
            def _(sp):
                sp.dma_start(w[:], w_tok).then_inc(w_loaded, 16)
                for c in range(CHUNKS):
                    if c >= 2:
                        sp.wait_ge(h_summed, 2 * (c - 1))
                    sp.dma_start(px[c % 2][:], patches[c]).then_inc(px_loaded[c % 2], 16)

            @block.tensor
            def _(pe):
                pe.wait_ge(w_loaded, 16)
                for c in range(CHUNKS):
                    pe.wait_ge(px_loaded[c % 2], 16 * (c // 2 + 1))
                    for half in range(2):
                        n = 2 * c + half
                        if n >= 4:
                            pe.wait_ge(h_copied, n - 3)
                        for k in range(PK):
                            mm = pe.matmul(acc[n % 4][:, :CT], w[:, k, half * HC:(half + 1) * HC],
                                           px[c % 2][:, k, :], start=k == 0, stop=k == PK - 1)
                        mm.then_inc(h_summed, 1)

            @block.scalar
            def _(act):
                act.dma_start(const["ident"][:], const["ident_d"]).then_inc(consts_loaded, 16)
                for n in range(2 * CHUNKS):
                    c, half = divmod(n, 2)
                    act.wait_ge(h_summed, n + 1)
                    act.activation(H[:, half, c * CT:(c + 1) * CT], acc[n % 4][:, :CT],
                                   ACT.Copy).then_inc(h_copied, 1)

            @block.vector
            def _(dve):
                dve.memset(const["mean"][:], 1.0 / C).then_inc(consts_set, 1)
                dve.wait_ge(consts_loaded, 16)
                for g in range(3):
                    rows = slice(32 * g, 32 * g + 32)
                    dve.tensor_copy(const["sel"][rows, :], const["ident"][rows, rows]).then_inc(consts_set, 1)


def norm_signals(nc, name):
    return {what: nc.alloc_semaphore(f"{name}_{what}")
            for what in ("mean_ready", "cent_ready", "sqr_ready", "var_ready", "rstd_steps", "out_steps")}


def normalise(nc, const, name, signals, past, src, dst, mode, gain=None, shift=None):
    rms = mode == "rms_add"
    with ExitStack() as ctx:
        mean_ps = [ctx.enter_context(nc.psum_tensor(f"{name}_mean{i}", [HC, 512], F32)) for i in range(2)]
        var_ps = [ctx.enter_context(nc.psum_tensor(f"{name}_var{i}", [HC, 512], F32)) for i in range(2)]
        cent = [ctx.enter_context(nc.sbuf_tensor(f"{name}_cent{i}", [HC, 2, CT], F32)) for i in range(2)]
        sqr = [ctx.enter_context(nc.sbuf_tensor(f"{name}_sqr{i}", [HC, 2, CT], F32)) for i in range(2)]
        rstd = [ctx.enter_context(nc.sbuf_tensor(f"{name}_rstd{i}", [HC, CT], F32)) for i in range(2)]
        mean_ready = signals["mean_ready"]
        cent_ready = signals["cent_ready"]
        sqr_ready = signals["sqr_ready"]
        var_ready = signals["var_ready"]
        rstd_steps = signals["rstd_steps"]
        out_steps = signals["out_steps"]
        outs = {"layer": 1, "layer_add": 4, "rms_add": 4}[mode]

        def piece(c):
            return slice(c * CT, (c + 1) * CT)

        def centred(c):
            return src[:, :, piece(c)] if rms else cent[c % 2][:]

        with nc.Block() as block:
            @block.tensor
            def _(pe):
                def mean(c):
                    if c >= 2:
                        pe.wait_ge(cent_ready, past + c - 1)
                    for half in range(2):
                        mm = pe.matmul(mean_ps[c % 2][:, :CT], const["mean"][:], src[:, half, piece(c)],
                                       start=half == 0, stop=half == 1)
                    mm.then_inc(mean_ready, 1)

                def var(c):
                    pe.wait_ge(sqr_ready, past + c + 1)
                    if c >= 2:
                        pe.wait_ge(rstd_steps, 2 * (past + c - 1))
                    for half in range(2):
                        mm = pe.matmul(var_ps[c % 2][:, :CT], const["mean"][:], sqr[c % 2][:, half, :],
                                       start=half == 0, stop=half == 1)
                    mm.then_inc(var_ready, 1)

                for c in range(CHUNKS + 1):
                    if c < CHUNKS and not rms:
                        mean(c)
                    if c >= 1:
                        var(c - 1)

            @block.scalar
            def _(act):
                act.preload_act_table_set(EXP_SET)
                for c in range(CHUNKS + 1):
                    if c < CHUNKS:
                        if not rms:
                            act.wait_ge(cent_ready, past + c + 1)
                        if c >= 2:
                            act.wait_ge(var_ready, past + c - 1)
                        act.activation(sqr[c % 2][:], centred(c), ACT.Square).then_inc(sqr_ready, 1)
                    if c >= 1:
                        b = (c - 1) % 2
                        act.wait_ge(var_ready, past + c)
                        if c >= 3:
                            act.wait_ge(out_steps, outs * (past + c - 2))
                        act.activation(rstd[b][:], var_ps[b][:, :CT], ACT.Ln, bias=EPS).then_inc(rstd_steps, 1)
                        act.wait_ge(rstd_steps, 2 * (past + c) - 1)
                        act.activation(rstd[b][:], rstd[b][:], ACT.Exp, scale=-0.5).then_inc(rstd_steps, 1)

            @block.vector
            def _(dve):
                def centre(c):
                    dve.wait_ge(mean_ready, past + c + 1)
                    if c >= 2:
                        dve.wait_ge(out_steps, outs * (past + c - 1))
                        dve.wait_ge(sqr_ready, past + c - 1)
                    dve.tensor_tensor(cent[c % 2][:], src[:, :, piece(c)],
                                      mean_ps[c % 2][:, None, :CT].to_broadcast([HC, 2, CT]),
                                      ALU.subtract).then_inc(cent_ready, 1)

                def output(c):
                    b = c % 2
                    dve.wait_ge(rstd_steps, 2 * (past + c) + 2)
                    if not rms:
                        dve.wait_ge(cent_ready, past + c + 1)
                    wide = rstd[b][:, None, :].to_broadcast([HC, 2, CT])
                    if mode == "layer":
                        dve.tensor_tensor(dst[:, :, piece(c)], cent[b][:], wide, ALU.mult).then_inc(out_steps, 1)
                        return
                    if rms and c >= 2:
                        dve.wait_ge(out_steps, outs * (past + c - 1))
                    for half in range(2):
                        dve.scalar_tensor_tensor(cent[b][:, half, :], centred(c)[:, half, :], gain[:, half:half + 1],
                                                 rstd[b][:], ALU.mult, ALU.mult).then_inc(out_steps, 1)
                    dve.wait_ge(out_steps, outs * (past + c) + 2)
                    if mode == "layer_add":
                        for half in range(2):
                            dve.scalar_tensor_tensor(dst[:, half, piece(c)], cent[b][:, half, :],
                                                     shift[:, half:half + 1], dst[:, half, piece(c)],
                                                     ALU.add, ALU.add).then_inc(out_steps, 1)
                    else:
                        for half in range(2):
                            dve.tensor_tensor(dst[:, half, piece(c)], cent[b][:, half, :], dst[:, half, piece(c)],
                                              ALU.add).then_inc(out_steps, 1)

                for c in range(CHUNKS + 1):
                    if c < CHUNKS and not rms:
                        centre(c)
                    if c >= 1:
                        output(c - 1)


class Banks:

    def __init__(self, order, steps):
        self.order, self.steps = order, steps

    @staticmethod
    def of(use):
        return 0 if use[0] == "B" else 1

    @staticmethod
    def kind(use):
        return ("after" if use[:3] == "out" else "early" if use == "rms" or use[:2] == "bm"
                else "scan" if use[0] in "BCz" else "ahead")

    def uses(self, k):
        kinds = {kind for kind, first, last in (("early", -2, self.steps - 3), ("ahead", -1, self.steps - 2),
                                                ("scan", 0, self.steps - 1), ("after", 1, self.steps))
                 if first <= k <= last}
        return [u for u in self.order if self.kind(u) in kinds]

    def count(self, k, bank, before=None):
        uses = self.uses(k)
        if before is not None:
            uses = uses[:uses.index(before)]
        return sum(self.of(u) == bank for u in uses)

    def index(self, use, k):
        b = self.of(use)
        if isinstance(k, int):
            return sum(self.count(i, b) for i in range(-2, k)) + self.count(k, b, use)
        before = sum(self.count(i, b) for i in (-2, -1, 0)) - self.count(1, b)
        return self.count(1, b) * k + (before + self.count(1, b, use))


def mamba(nc, const, name, layers, weights, X, out, direction=None, bm=None):
    inner = direction is None
    STEPS = layers * CHUNKS
    NDA, NH, NHC, NCB = (4 if inner else 2), 4, 4, 4
    extra = {0: "in0", 1: "in1", 2: "in2", 3: "z0", 4: "z1", 5: "z2", 7: "low", 8: "dt0", 9: "dt1", 10: "dt2",
             11: "out0", 12: "out1", 13: "rms" if inner else "bm0"}
    if not inner:
        extra[14] = "bm1"
    banks = Banks([u for n in range(NS) for u in (f"B{n}", f"C{n}", extra.get(n)) if u], STEPS)

    with ExitStack() as ctx:
        def sb(what, shape, dt=F32):
            return ctx.enter_context(nc.sbuf_tensor(f"{name}_{what}", shape, dt))

        def sem(what):
            return nc.alloc_semaphore(f"{name}_{what}")

        par = sb("par", [128, layers, P_END])
        par_core = [sb(f"par_core{i}", [128, N_CORE]) for i in range(2)]
        par_pre = sb("par_pre", [128, N_PRE])
        in_w = sb("in_w", [HC, 2, 6 * 128])
        xp_w = sb("xp_w", [128, DT, LOW])
        dt_w = sb("dt_w", [RANK, DT * 128])
        out_w = sb("out_w", [128, DT, C])
        hn = [sb(f"hn{i}", [HC, 2, CT]) for i in range(2)]
        conv_in = sb("conv_in", [128, DT, CS, LEN + 3])
        conv = sb("conv", [128, DT, CT])
        u = [sb(f"u{i}", [128, DT, CT]) for i in range(2)]
        gate = [sb(f"gate{i}", [128, DT, CT]) for i in range(2)]
        dt = [sb(f"dt{i}", [128, DT, CT]) for i in range(2)]
        dtu = [sb(f"dtu{i}", [128, DT, CT]) for i in range(2)]
        bc_parts = [sb(f"bc_parts{i}", [96, CT], BF16) for i in range(2)]
        bc = sb("bc", [32, CT])
        bc_head = sb("bc_head", [32, CT], BF16)
        bc_mid = sb("bc_mid", [32, CT], BF16)
        series = sb("series", [128, DT, CT])
        dt_low = sb("dt_low", [RANK, CT])
        decay = [sb(f"decay{i}", [128, DT, CT]) for i in range(NDA)]
        state = [sb(f"state{i}", [128, DT, CT]) for i in range(NH)]
        cstate = [sb(f"cstate{i}", [128, DT, CT]) for i in range(NHC)]
        c_wide = [sb(f"c_wide{i}", [128, CT]) for i in range(NCB)]
        y_out = sb("y_out", [128, DT, CT])
        if inner:
            par_norm = sb("par_norm", [HC, 2])
            sqr = sb("sqr", [HC, 2, CT])
            rstd = sb("rstd", [HC, CT])
        else:
            bm_w = sb("bm_w", [HC, 2, C])
            bm_b = sb("bm_b", [HC, 2])
        y_ps = ctx.enter_context(nc.psum_tensor(f"{name}_y_ps", [128, DT, 512], F32))
        dbu_ps = ctx.enter_context(nc.psum_tensor(f"{name}_dbu_ps", [128, 3 * 512], F32))
        dbu = dbu_ps[:, :DT * CT]
        bank = [ctx.enter_context(nc.psum_tensor(f"{name}_bank{i}", [128, 512], F32)) for i in range(2)]

        filled = [sem(f"bank{i}_filled") for i in range(2)]
        drained = [sem(f"bank{i}_drained") for i in range(2)]
        par_loaded, par_made, par_core_ready, par_pre_ready = map(
            sem, ("par_loaded", "par_made", "par_core_ready", "par_pre_ready"))
        pre_w_loaded, z_w_loaded, out_w_loaded, zeros_set = map(
            sem, ("pre_w_loaded", "z_w_loaded", "out_w_loaded", "zeros_set"))
        sqr_ready, rstd_steps, hn_steps = map(sem, ("sqr_ready", "rstd_steps", "hn_steps"))
        conv_steps, u_ready, gate_ready, rest_ready = map(sem, ("conv_steps", "u_ready", "gate_ready", "rest_ready"))
        mid_ready, parts_ready, dt_arg_ready, dt_act_steps = map(
            sem, ("mid_ready", "parts_ready", "dt_arg_ready", "dt_act_steps"))
        dt_steps, dt_ready, dtu_ready = map(sem, ("dt_steps", "dt_ready", "dtu_ready"))
        decay_ready, state_ready, cstate_ready, y_summed = map(
            sem, ("decay_ready", "state_ready", "cstate_ready", "y_summed"))
        y_steps, y_gated, tap_ready, head_ready = map(sem, ("y_steps", "y_gated", "tap_ready", "head_ready"))

        def layer_of(k):
            return k // CHUNKS

        def wait_filled(eng, use, k):
            eng.wait_ge(filled[banks.of(use)], banks.index(use, k) + 1)

        def wait_drained(eng, use, k):
            eng.wait_ge(drained[banks.of(use)], banks.index(use, k) + 1)

        def drain(ins, use):
            ins.then_inc(drained[banks.of(use)], 1)

        def ps(use):
            return bank[banks.of(use)]

        def run(eng, step):
            step(0, 0, after=False, ahead=True, early=True)
            step(1, 1, after=True, ahead=True, early=True)
            with eng.Fori(1, STEPS // 2 - 1) as j:
                step(2 * j, 0, after=True, ahead=True, early=True)
                step(2 * j + 1, 1, after=True, ahead=True, early=True)
            step(STEPS - 2, 0, after=True, ahead=True, early=False)
            step(STEPS - 1, 1, after=True, ahead=False, early=False)

        def start(early, ahead):
            for n in range(NS):
                early(n, -2, 0, 0)
            for n in range(NS):
                ahead(n, -1, 0, 0)
                early(n, -1, 1, 1)

        with nc.Block() as block:
            @block.sync
            def _(sp):
                sp.dma_start(par[:], weights["par"]).then_inc(par_loaded, 16)

                def load_in(layer, part, done):
                    cols = slice(part * DT * 128, (part + 1) * DT * 128)
                    src = weights["in_w"][bass.ds(layer, 1), :, :, cols].rearrange("a p b n -> p (a b) n")
                    sp.dma_start(in_w[:, :, cols], src).then_inc(done, 16)

                def load_pre(layer):
                    load_in(layer, 0, pre_w_loaded)
                    for dst, w in ((xp_w, "xp_w"), (dt_w, "dt_w")):
                        src = weights[w][bass.ds(layer, 1)].rearrange("a p n -> p (a n)")
                        flat = dst[:] if len(dst.shape) == 2 else dst[:].rearrange("p a b -> p (a b)")
                        sp.dma_start(flat, src).then_inc(pre_w_loaded, 16)

                def load_out(layer):
                    sp.dma_start(out_w[:].rearrange("p a b -> p (a b)"),
                                 weights["out_w"][bass.ds(layer, 1)].rearrange("a p n -> p (a n)")
                                 ).then_inc(out_w_loaded, 16)

                if not inner:
                    sp.dma_start(bm_w[:], bm["w"]).then_inc(pre_w_loaded, 16)
                    sp.dma_start(bm_b[:], bm["b"]).then_inc(pre_w_loaded, 16)
                load_pre(0)
                load_in(0, 1, z_w_loaded)
                load_out(0)
                if layers > 1:
                    with sp.Fori(1, layers) as l:
                        wait_filled(sp, "dt2", l * CHUNKS - 2)
                        load_pre(l)
                        wait_filled(sp, "z2", l * CHUNKS - 1)
                        load_in(l, 1, z_w_loaded)
                        wait_filled(sp, "out1", l * CHUNKS)
                        load_out(l)

            n_pre_w = 16 * (3 if inner else 5)

            @block.tensor
            def _(pe):
                def take(use, k):
                    before = banks.index(use, k)
                    if not (isinstance(before, int) and before == 0):
                        pe.wait_ge(drained[banks.of(use)], before)

                def give(mm, use):
                    mm.then_inc(filled[banks.of(use)], 1)

                def sum_y(k, n, tiles=range(DT)):
                    if 0 in tiles:
                        if n == 0 and not (isinstance(k, int) and k == 0):
                            pe.wait_ge(y_steps, 3 * k)
                        pe.wait_ge(cstate_ready, NS * k + n + 1)
                    for t in tiles:
                        mm = pe.matmul(y_ps[:, t, :CT], const["ident"][:], cstate[n % NHC][:, t, :],
                                       start=n == 0, stop=n == NS - 1)
                    if DT - 1 in tiles:
                        mm.then_inc(y_summed, 1)

                def in_product(use, m, k, b):
                    take(use, k)
                    for half in range(2):
                        mm = pe.matmul(ps(use)[:, :CT], in_w[:, half, m * 128:(m + 1) * 128],
                                       hn[b][:, half, :], start=half == 0, stop=half == 1)
                    give(mm, use)

                def early(n, k, k2, b2):
                    if n == 13 and inner:
                        pe.wait_ge(sqr_ready, k2 + 1)
                        take("rms", k)
                        for half in range(2):
                            mm = pe.matmul(ps("rms")[:HC, :CT], const["mean"][:], sqr[:, half, :],
                                           start=half == 0, stop=half == 1)
                        give(mm, "rms")
                    if n in (13, 14) and not inner:
                        m = n - 13
                        if m == 0:
                            pe.wait_ge(pre_w_loaded, n_pre_w)
                        take(f"bm{m}", k)
                        for half in range(2):
                            mm = pe.matmul(ps(f"bm{m}")[:HC, :CT], bm_w[:, half, m * HC:(m + 1) * HC],
                                           X[:, half, bass.ds(chunk_of(k2), CT)], start=half == 0, stop=half == 1)
                        give(mm, f"bm{m}")

                def ahead(n, k, k1, b1):
                    if n in (0, 1, 2):
                        if n == 0:
                            pe.wait_ge(pre_w_loaded, n_pre_w * (layer_of(k1) + 1))
                            if inner:
                                pe.wait_ge(hn_steps, 2 * (k1 + 1))
                            else:
                                wait_drained(pe, "bm1", k1 - 2)
                        in_product(f"in{n}", n, k, b1)
                    if n == 7:
                        pe.wait_ge(u_ready, k1 + 1)
                        take("low", k)
                        for t in range(DT):
                            mm = pe.matmul(ps("low")[:LOW, :CT], xp_w[:, t, :], u[b1][:, t, :],
                                           start=t == 0, stop=t == DT - 1)
                        give(mm, "low")
                    if n in (8, 9, 10):
                        t = n - 8
                        if t == 0:
                            wait_drained(pe, "low", k)
                        take(f"dt{t}", k)
                        mm = pe.matmul(ps(f"dt{t}")[:, :CT], dt_w[:, t * 128:(t + 1) * 128], dt_low[:],
                                       start=True, stop=True)
                        give(mm, f"dt{t}")

                def after(n, k, b):
                    if n in (11, 12):
                        half = n - 11
                        if half == 0:
                            pe.wait_ge(y_gated, k)
                            pe.wait_ge(out_w_loaded, 16 * (layer_of(k - 1) + 1))
                        take(f"out{half}", k)
                        for t in range(DT):
                            mm = pe.matmul(ps(f"out{half}")[:HC, :CT], out_w[:, t, half * HC:(half + 1) * HC],
                                           y_out[:, t, :], start=t == 0, stop=t == DT - 1)
                        give(mm, f"out{half}")

                def spread(use, row, k, b):
                    take(use, k)
                    give(pe.matmul(ps(use)[:, :CT], const["sel"][:, row:row + 1].to_broadcast([96, 128]),
                                   bc_parts[b][:], start=True, stop=True), use)

                def step(k, b, **parts):
                    for n in range(NS):
                        spread(f"C{n}", NS + n, k, b)
                        sums = [(k - 1, NS - 3 + n)] if n < 3 and parts["after"] else [
                            (k, m) for m in {4: (0,), 5: (1,), 6: (2, 3)}.get(n, (n - 3,) if n > 6 else ())]
                        for of, m in sums:
                            sum_y(of, m, range(1))
                        if n == 3:
                            pe.wait_ge(z_w_loaded, 16 * (layer_of(k) + 1))
                        if n in (3, 4, 5):
                            in_product(f"z{n - 3}", n, k, b)
                        if parts["after"]:
                            after(n, k, b)
                        if parts["ahead"]:
                            ahead(n, k, k + 1, 1 - b)
                        if parts["early"]:
                            early(n, k, k + 2, b)
                        if n < NS - 1:
                            spread(f"B{n + 1}", n + 1, k, b)
                        elif parts["ahead"]:
                            pe.wait_ge(parts_ready, k + 2)
                            spread("B0", 0, k + 1, 1 - b)
                        for of, m in sums:
                            sum_y(of, m, range(1, DT))

                start(early, ahead)
                pe.wait_ge(parts_ready, 1)
                spread("B0", 0, 0, 0)
                run(pe, step)
                for n in (NS - 3, NS - 2, NS - 1):
                    sum_y(STEPS - 1, n)
                for n in (11, 12):
                    after(n, STEPS, 0)

            @block.scalar
            def _(act):
                def silu(out_, in_, done):
                    act.activation(out_[:], in_[:], ACT.Silu).then_inc(done, 1)

                def early(n, k, k2, b2):
                    if n == 12 and inner:
                        if not isinstance(k2, int) or k2 > 0:
                            act.wait_ge(hn_steps, 2 * k2)
                        act.activation(par_norm[:], par[:HC, bass.ds(layer_of(k2), 1), P_NW:P_END].rearrange(
                            "p a n -> p (a n)"), ACT.Copy)
                        act.activation(sqr[:], X[:, :, bass.ds(chunk_of(k2), CT)], ACT.Square
                                       ).then_inc(sqr_ready, 1)
                    if n == 14 and inner:
                        wait_filled(act, "rms", k)
                        drain(act.activation(rstd[:], ps("rms")[:HC, :CT], ACT.Ln, bias=EPS), "rms")
                        wait_drained(act, "rms", k)
                        act.activation(rstd[:], rstd[:], ACT.Exp, scale=-0.5).then_inc(rstd_steps, 1)
                    if n in (14, 15) and not inner:
                        m = n - 14
                        wait_filled(act, f"bm{m}", k)
                        got = seqs(ps(f"bm{m}")[:HC, :CT])
                        if direction == "backward":
                            got = got[:, :, ::-1]
                        drain(act.activation(seqs(hn[b2][:, m, :]), got, ACT.Identity, bias=bm_b[:, m:m + 1]),
                              f"bm{m}")

                def ahead(n, k, k1, b1):
                    if n == 0:
                        act.activation(par_pre[:], par[:, bass.ds(layer_of(k1), 1), P_CW:P_NW].rearrange(
                            "p a n -> p (a n)"), ACT.Copy).then_inc(par_pre_ready, 1)
                    if n in (1, 2, 3):
                        m = n - 1
                        wait_filled(act, f"in{m}", k)
                        if m == 0:
                            act.wait_ge(par_pre_ready, k1 + 1)
                        drain(act.activation(conv_in[:, m, :, 3:], seqs(ps(f"in{m}")[:, :CT]), ACT.Copy),
                              f"in{m}")
                        wait_drained(act, f"in{m}", k)
                        act.activation(seqs(conv[:, m, :]), conv_in[:, m, :, 3:], ACT.Identity,
                                       scale=par_pre[:, 4 * m + 3:4 * m + 4],
                                       bias=par_pre[:, P_CB - P_CW + m:P_CB - P_CW + m + 1]).then_inc(tap_ready, 1)
                    if n == 6:
                        act.wait_ge(conv_steps, 9 * (k1 + 1))
                        silu(u[b1], conv, u_ready)
                    if n == 8:
                        wait_filled(act, "low", k)
                        got = ps("low")[:, :CT]
                        act.activation(bc[:], got[:32], ACT.Copy)
                        drain(act.activation(dt_low[:], got[64:LOW], ACT.Copy), "low")
                        wait_drained(act, "low", k)
                        act.activation(bc_head[:], bc[:], ACT.Copy).then_inc(head_ready, 1)
                        act.activation(bc_parts[b1][:32, :], bc[:], ACT.Copy).then_inc(head_ready, 1)
                    if n in (9, 10, 11):
                        t = n - 9
                        if t == 0:
                            act.wait_ge(u_ready, k1 + 1)
                        wait_filled(act, f"dt{t}", k)
                        drain(act.activation(conv[:, t, :], ps(f"dt{t}")[:, :CT], ACT.Identity,
                                             bias=par_pre[:, P_DTB - P_CW + t:P_DTB - P_CW + t + 1]), f"dt{t}")
                    if n == 10:
                        act.wait_ge(rest_ready, k1 + 1)
                        act.activation(bc_parts[b1][32:64, :], bc[:], ACT.Copy)
                        act.activation(bc_mid[:], bc[:], ACT.Copy).then_inc(mid_ready, 1)
                    if n == 12:
                        act.wait_ge(dt_arg_ready, k1 + 1)
                        act.activation(dt[b1][:], dt[b1][:], ACT.Exp, bias=LOG_SMALL).then_inc(dt_act_steps, 1)
                        act.activation(par_core[b1][:], par[:, bass.ds(layer_of(k1), 1), P_A:P_CW].rearrange(
                            "p a n -> p (a n)"), ACT.Copy).then_inc(par_core_ready, 1)
                        act.wait_ge(dt_act_steps, 2 * k1 + 1)
                        act.activation(dtu[b1][:], dt[b1][:], ACT.Ln, scale=1.0 / (1.0 + SMALL),
                                       bias=1.0 / (1.0 + SMALL)).then_inc(dt_act_steps, 1)

                def step(k, b, **parts):
                    for n in range(NS):
                        if n == 0:
                            act.wait_ge(dt_ready, k + 1)
                            act.wait_ge(par_core_ready, k + 1)
                        if not (isinstance(k, int) and NS * k + n < NDA):
                            act.wait_ge(state_ready, NS * k + n + 1 - NDA)
                        for t in range(DT):
                            last = act.activation(seqs(decay[n % NDA][:, t, :])[:, :, 1:],
                                                  seqs(dt[b][:, t, :])[:, :, 1:], ACT.Exp,
                                                  scale=par_core[b][:, NS * t + n:NS * t + n + 1])
                        last.then_inc(decay_ready, 1)
                        if n in (4, 5, 6):
                            wait_filled(act, f"z{n - 4}", k)
                            drain(act.activation(gate[b][:, n - 4, :], ps(f"z{n - 4}")[:, :CT], ACT.Copy),
                                  f"z{n - 4}")
                        if parts["ahead"] and n != 6:
                            ahead(n, k, k + 1, 1 - b)
                        if parts["early"]:
                            early(n, k, k + 2, b)
                        wait_filled(act, f"C{n}", k)
                        if not (isinstance(k, int) and NS * k + n < NCB):
                            act.wait_ge(cstate_ready, NS * k + n + 1 - NCB)
                        drain(act.activation(c_wide[n % NCB][:], ps(f"C{n}")[:, :CT], ACT.Copy), f"C{n}")
                        if n == 6:
                            if parts["ahead"]:
                                ahead(n, k, k + 1, 1 - b)
                            wait_drained(act, "z2", k)
                            silu(gate[b], gate[b], gate_ready)
                            act.preload_act_table_set(EXP_SET)

                act.preload_act_table_set(EXP_SET)
                act.wait_ge(par_loaded, 16)
                act.wait_ge(zeros_set, 1)
                a_log = par[:, :, P_A:P_D]
                act.activation(a_log, a_log, ACT.Exp).then_inc(par_made, 1)
                act.wait_ge(par_made, 1)
                act.activation(a_log, a_log, ACT.Copy, scale=-1.0).then_inc(par_made, 1)
                dt_bias = par[:, :, P_DTB:P_NW]
                act.activation(dt_bias, dt_bias, ACT.Identity, bias=-LOG_SMALL).then_inc(par_made, 1)
                act.wait_ge(par_made, 3)
                if not inner:
                    act.wait_ge(pre_w_loaded, n_pre_w)
                for n in range(NS):
                    early(n, -2, 0, 0)
                for n in range(NS):
                    ahead(n, -1, 0, 0)
                    if n == 6:
                        act.preload_act_table_set(EXP_SET)
                    early(n, -1, 1, 1)
                run(act, step)

            @block.vector
            def _(dve):
                def early(n, k, k2, b2):
                    if n == 15 and inner:
                        dve.wait_ge(rstd_steps, k2 + 1)
                        for half in range(2):
                            dve.scalar_tensor_tensor(hn[b2][:, half, :], X[:, half, bass.ds(chunk_of(k2), CT)],
                                                     par_norm[:, half:half + 1], rstd[:], ALU.mult, ALU.mult
                                                     ).then_inc(hn_steps, 1)

                def ahead(n, k, k1, b1):
                    if n in (2, 4, 5):
                        t = {2: 0, 4: 1, 5: 2}[n]
                        for tap in range(3):
                            if tap == 0:
                                dve.wait_ge(tap_ready, DT * k1 + t + 1)
                            else:
                                dve.wait_ge(conv_steps, 9 * k1 + 3 * t + tap)
                            dve.scalar_tensor_tensor(seqs(conv[:, t, :]), conv_in[:, t, :, tap:tap + LEN],
                                                     par_pre[:, 4 * t + tap:4 * t + tap + 1],
                                                     seqs(conv[:, t, :]), ALU.mult, ALU.add).then_inc(conv_steps, 1)
                    if n == 8:
                        dve.wait_ge(head_ready, 2 * (k1 + 1))
                        dve.tensor_tensor(bc[:], bc[:], bc_head[:], ALU.subtract).then_inc(rest_ready, 1)
                    if n == 11:
                        dve.wait_ge(mid_ready, k1 + 1)
                        dve.tensor_tensor(bc_parts[b1][64:96, :], bc[:], bc_mid[:], ALU.subtract
                                          ).then_inc(parts_ready, 1)
                        wait_drained(dve, "dt2", k)
                        dve.tensor_scalar(dt[b1][:], conv[:], 40.0, None, ALU.min).then_inc(dt_arg_ready, 1)
                    if n == 12:
                        dve.wait_ge(dt_act_steps, 2 * k1 + 2)
                        dve.tensor_scalar(dt[b1][:], dt[b1][:], SMALL, 0.5 ** 0.5, ALU.min, ALU.mult
                                          ).then_inc(dt_steps, 1)
                        dve.wait_ge(dt_steps, 3 * k1 + 1)
                        dve.scalar_tensor_tensor(series[:], dt[b1][:], -2.0 ** 0.5, dt[b1][:], ALU.add,
                                                 ALU.mult).then_inc(dt_steps, 1)
                        dve.scalar_tensor_tensor(conv[:], dtu[b1][:], 0.0, conv[:], ALU.max, ALU.max
                                                 ).then_inc(dt_steps, 1)

                def collect(n, k, b):
                    if n == 3:
                        dve.wait_ge(y_summed, NS * k)
                        for t in range(DT):
                            dve.scalar_tensor_tensor(y_out[:, t, :], u[1 - b][:, t, :],
                                                     par_core[1 - b][:, P_D + t:P_D + t + 1],
                                                     y_ps[:, t, :CT], ALU.mult, ALU.add).then_inc(y_steps, 1)
                    if n in (12, 13):
                        half = n - 12
                        wait_filled(dve, f"out{half}", k)
                        got = ps(f"out{half}")[:HC, :CT]
                        dst = out[:, half, bass.ds(chunk_of(k - 1), CT)]
                        if direction == "forward":
                            drain(dve.tensor_copy(dst, got), f"out{half}")
                        elif direction == "backward":
                            drain(dve.tensor_tensor(seqs(dst), seqs(dst), seqs(got)[:, :, ::-1], ALU.add),
                                  f"out{half}")
                        else:
                            drain(dve.tensor_tensor(dst, dst, got, ALU.add), f"out{half}")

                def step(k, b, **parts):
                    for n in range(NS):
                        if n == 0:
                            dve.wait_ge(dtu_ready, k + 1)
                        i = NS * k + n
                        if parts["after"]:
                            collect(n, k, b)
                        wait_filled(dve, f"B{n}", k)
                        if not (isinstance(i, int) and i == 0):
                            dve.wait_ge(state_ready, i)
                        drain(dve.tensor_tensor(dbu.rearrange("p (t s) -> p t s", t=DT), dtu[b][:],
                                                ps(f"B{n}")[:, None, :CT].to_broadcast([128, DT, CT]),
                                                ALU.mult), f"B{n}")
                        wait_drained(dve, f"B{n}", k)
                        dve.wait_ge(decay_ready, i + 1)
                        if not (isinstance(i, int) and i < NH):
                            dve.wait_ge(cstate_ready, i + 1 - NH)
                        dve.tensor_tensor_scan(state[n % NH][:].rearrange("p t s -> p (t s)"),
                                               decay[n % NDA][:].rearrange("p t s -> p (t s)"), dbu, 0.0,
                                               ALU.mult, ALU.add).then_inc(state_ready, 1)
                        if parts["ahead"]:
                            ahead(n, k, k + 1, 1 - b)
                        if parts["early"]:
                            early(n, k, k + 2, b)

                dve.memset(conv_in[:], 0.0)
                for d in decay:
                    last = dve.memset(d[:], 0.0)
                last.then_inc(zeros_set, 1)
                start(early, ahead)
                run(dve, step)
                for n in (3, 12, 13):
                    collect(n, STEPS, 0)

            @block.gpsimd
            def _(pool):
                def ahead(n, k, k1, b1):
                    if n == 12:
                        pool.wait_ge(dt_steps, 3 * k1 + 3)
                        pool.tensor_tensor(dt[b1][:], conv[:], series[:], ALU.subtract).then_inc(dt_ready, 1)
                    if n == 13:
                        pool.wait_ge(dt_ready, k1 + 1)
                        pool.tensor_tensor(dtu[b1][:], dt[b1][:], u[b1][:], ALU.mult).then_inc(dtu_ready, 1)

                def after(n, k, b):
                    if n == 4:
                        pool.wait_ge(y_steps, 3 * k)
                        pool.wait_ge(gate_ready, k)
                        pool.tensor_tensor(y_out[:], y_out[:], gate[1 - b][:], ALU.mult).then_inc(y_gated, 1)

                def step(k, b, **parts):
                    for n in range(NS):
                        i = NS * k + n
                        pool.wait_ge(state_ready, i + 1)
                        wait_drained(pool, f"C{n}", k)
                        if not (isinstance(i, int) and i < NHC):
                            pool.wait_ge(y_summed, i + 1 - NHC)
                        pool.tensor_tensor(cstate[n % NHC][:], state[n % NH][:],
                                           c_wide[n % NCB][:, None, :].to_broadcast([128, DT, CT]),
                                           ALU.mult).then_inc(cstate_ready, 1)
                        if parts["after"]:
                            after(n, k, b)
                        if parts["ahead"]:
                            ahead(n, k, k + 1, 1 - b)

                for n in range(NS):
                    ahead(n, -1, 0, 0)
                run(pool, step)
                after(4, STEPS, 0)


def project(nc, name, w_d, b_d, src, add, gain_d, shift_d, gain, shift):
    with ExitStack() as ctx:
        w = ctx.enter_context(nc.sbuf_tensor(f"{name}_w", [HC, 2, C], F32))
        b = ctx.enter_context(nc.sbuf_tensor(f"{name}_b", [HC, 2], F32))
        acc = [[ctx.enter_context(nc.psum_tensor(f"{name}_ps{i}{h}", [HC, 512], F32)) for h in range(2)]
               for i in range(2)]
        loaded = nc.alloc_semaphore(f"{name}_loaded")
        summed = nc.alloc_semaphore(f"{name}_summed")
        added = nc.alloc_semaphore(f"{name}_added")
        with nc.Block() as block:
            @block.sync
            def _(sp):
                for dst, d in ((w, w_d), (b, b_d), (gain, gain_d), (shift, shift_d)):
                    sp.dma_start(dst[:], d).then_inc(loaded, 16)

            @block.tensor
            def _(pe):
                pe.wait_ge(loaded, 64)
                for c in range(CHUNKS):
                    if c >= 2:
                        pe.wait_ge(added, 2 * (c - 1))
                    for m in range(2):
                        for half in range(2):
                            mm = pe.matmul(acc[c % 2][m][:, :CT], w[:, half, m * HC:(m + 1) * HC],
                                           src[:, half, c * CT:(c + 1) * CT], start=half == 0, stop=half == 1)
                    mm.then_inc(summed, 1)

            @block.vector
            def _(dve):
                dve.wait_ge(loaded, 64)
                for c in range(CHUNKS):
                    dve.wait_ge(summed, c + 1)
                    for m in range(2):
                        dve.scalar_tensor_tensor(src[:, m, c * CT:(c + 1) * CT], acc[c % 2][m][:, :CT],
                                                 b[:, m:m + 1], add[:, m, c * CT:(c + 1) * CT],
                                                 ALU.add, ALU.add).then_inc(added, 1)


def route(nc, const, wg_d, lower_d, XN, gates):
    with ExitStack() as ctx:
        def sb(what, shape):
            return ctx.enter_context(nc.sbuf_tensor(f"route_{what}", shape, F32))

        def sem(what):
            return nc.alloc_semaphore(f"route_{what}")

        wg = sb("wg", [HC, 2, EXPERTS])
        lower = sb("lower", [128, EXPERTS * EXPERTS])
        prob = sb("prob", [BLK, NBLK, EXPERTS])
        col = sb("col", [BLK, NBLK])
        inv = sb("inv", [BLK, NBLK])
        before = sb("before", [BLK, NBLK, EXPERTS, EXPERTS])
        tie = sb("tie", [BLK, NBLK, EXPERTS, EXPERTS])
        rank = sb("rank", [BLK, NBLK, EXPERTS])
        logit_ps = ctx.enter_context(nc.psum_tensor("route_logit_ps", [BLK, NBLK, 16], F32))
        turn_ps = [ctx.enter_context(nc.psum_tensor(f"route_turn_ps{i}", [EXPERTS, 512], F32)) for i in range(4)]
        loaded, logits_ready, shifted_ready, exp_ready = map(
            sem, ("loaded", "logits_ready", "shifted_ready", "exp_ready"))
        chain, weights_ready, turned, copied = map(sem, ("chain", "weights_ready", "turned", "copied"))
        per_bank = CT // BLK
        logits = logit_ps[:, :, :EXPERTS]

        with nc.Block() as block:
            @block.sync
            def _(sp):
                sp.dma_start(wg[:], wg_d).then_inc(loaded, 16)
                sp.dma_start(lower[:], lower_d).then_inc(loaded, 16)

            @block.tensor
            def _(pe):
                pe.wait_ge(loaded, 32)
                for t in range(NBLK):
                    for half in range(2):
                        mm = pe.matmul(logits[:, t, :], XN[:, half, t * BLK:(t + 1) * BLK], wg[:, half, :],
                                       start=half == 0, stop=half == 1)
                mm.then_inc(logits_ready, 1)
                pe.wait_ge(weights_ready, 1)
                for t in range(NBLK):
                    c, i = divmod(t, per_bank)
                    if c >= 4 and i == 0:
                        pe.wait_ge(copied, c - 3)
                    mm = pe.matmul(turn_ps[c % 4][:, i * BLK:(i + 1) * BLK], prob[:, t, :],
                                   const["ident"][:BLK, :BLK], start=True, stop=True)
                    if i == per_bank - 1:
                        mm.then_inc(turned, 1)

            @block.scalar
            def _(act):
                act.preload_act_table_set(EXP_SET)
                act.wait_ge(shifted_ready, 1)
                act.activation(prob[:], prob[:], ACT.Exp).then_inc(exp_ready, 1)
                for c in range(CHUNKS):
                    act.wait_ge(turned, c + 1)
                    act.activation(gates[:, c * CT:(c + 1) * CT], turn_ps[c % 4][:, :CT], ACT.Copy
                                   ).then_inc(copied, 1)

            @block.vector
            def _(dve):
                done = [0]

                def then(ins):
                    ins.then_inc(chain, 1)
                    done[0] += 1
                    dve.wait_ge(chain, done[0])

                def over_experts(t):
                    return t[:, :, None].to_broadcast([BLK, NBLK, EXPERTS])

                pair = [BLK, NBLK, EXPERTS, EXPERTS]
                dve.wait_ge(logits_ready, 1)
                then(dve.tensor_reduce(col[:], logits, AX.X, ALU.max))
                dve.tensor_tensor(prob[:], logits, over_experts(col), ALU.subtract).then_inc(shifted_ready, 1)
                dve.wait_ge(exp_ready, 1)
                then(dve.tensor_reduce(col[:], prob[:], AX.X, ALU.add))
                then(dve.reciprocal(inv[:], col[:]))
                then(dve.tensor_tensor(prob[:], prob[:], over_experts(inv), ALU.mult))
                own = prob[:, :, :, None].to_broadcast(pair)
                other = prob[:, :, None, :].to_broadcast(pair)
                then(dve.tensor_tensor(before[:], other, own, ALU.is_gt))
                then(dve.tensor_tensor(tie[:], other, own, ALU.is_equal))
                dve.wait_ge(loaded, 32)
                flat = tie[:].rearrange("p b e f -> p b (e f)")
                then(dve.tensor_tensor(flat, flat, lower[:BLK, None, :].to_broadcast(
                    [BLK, NBLK, EXPERTS * EXPERTS]), ALU.mult))
                then(dve.tensor_tensor(before[:], before[:], tie[:], ALU.add))
                then(dve.tensor_reduce(rank[:], before[:], AX.X, ALU.add))
                then(dve.scalar_tensor_tensor(prob[:], rank[:], 1.5, prob[:], ALU.is_lt, ALU.mult))
                then(dve.tensor_reduce(col[:], prob[:], AX.X, ALU.add))
                then(dve.reciprocal(inv[:], col[:]))
                dve.tensor_tensor(prob[:], prob[:], over_experts(inv), ALU.mult).then_inc(weights_ready, 1)


def experts(nc, const, fc_d, proj_d, XN, gates, H):
    TILES = EXPERTS * HT
    LAG, NHID = 2, 4
    with ExitStack() as ctx:
        fc = ctx.enter_context(nc.sbuf_tensor("moe_fc", [HC, EXPERTS, 2, HID], F32))
        proj = ctx.enter_context(nc.sbuf_tensor("moe_proj", [128, EXPERTS, HT, C], F32))
        hid = [ctx.enter_context(nc.sbuf_tensor(f"moe_hid{i}", [128, CT], F32)) for i in range(NHID)]
        gate = [ctx.enter_context(nc.sbuf_tensor(f"moe_gate{i}", [HC, CT], F32)) for i in range(2)]
        part = [ctx.enter_context(nc.sbuf_tensor(f"moe_part{i}", [HC, 2, CT], F32)) for i in range(2)]
        hid_ps = [ctx.enter_context(nc.psum_tensor(f"moe_hid_ps{i}", [128, 512], F32)) for i in range(3)]
        gate_ps = ctx.enter_context(nc.psum_tensor("moe_gate_ps", [HC, 512], F32))
        out_ps = [ctx.enter_context(nc.psum_tensor(f"moe_out_ps{i}", [HC, 2, 512], F32)) for i in range(2)]
        w_loaded = [nc.alloc_semaphore(f"moe_w_loaded{e}") for e in range(EXPERTS)]
        hid_summed = nc.alloc_semaphore("moe_hid_summed")
        hid_ready = nc.alloc_semaphore("moe_hid_ready")
        tile_used = nc.alloc_semaphore("moe_tile_used")
        gate_spread = nc.alloc_semaphore("moe_gate_spread")
        gate_ready = nc.alloc_semaphore("moe_gate_ready")
        part_ready = nc.alloc_semaphore("moe_part_ready")
        part_added = nc.alloc_semaphore("moe_part_added")

        def first(c):
            return isinstance(c, int) and c == 0

        def run(eng, chunk):
            chunk(0)
            with eng.Fori(1, CHUNKS) as c:
                chunk(c)

        with nc.Block() as block:
            @block.sync
            def _(sp):
                for e in range(EXPERTS):
                    sp.dma_start(fc[:, e], fc_d[:, e]).then_inc(w_loaded[e], 16)
                    sp.dma_start(proj[:, e], proj_d[:, e]).then_inc(w_loaded[e], 16)

            @block.tensor
            def _(pe):
                def chunk(c):
                    for i in range(TILES + LAG):
                        if i < TILES:
                            e, t = divmod(i, HT)
                            if t == 0:
                                if first(c):
                                    pe.wait_ge(w_loaded[e], 32)
                                if not (first(c) and e == 0):
                                    pe.wait_ge(gate_ready, EXPERTS * c + e)
                            if not (first(c) and i < 3):
                                pe.wait_ge(hid_ready, TILES * c + i - 2)
                            for half in range(2):
                                mm = pe.matmul(hid_ps[i % 3][:, :CT], fc[:, e, half, t * 128:(t + 1) * 128],
                                               XN[:, half, bass.ds(c * CT, CT)], start=half == 0, stop=half == 1)
                            mm.then_inc(hid_summed, 1)
                            if t == 0:
                                pe.matmul(gate_ps[:, :CT], const["ident"][:EXPERTS, e:e + 1].to_broadcast(
                                    [EXPERTS, HC]), gates[:, bass.ds(c * CT, CT)], start=True, stop=True
                                          ).then_inc(gate_spread, 1)
                        if i >= LAG:
                            e, t = divmod(i - LAG, HT)
                            pe.wait_ge(hid_ready, TILES * c + i - LAG + 1)
                            if t == 0 and not (first(c) and e < 2):
                                pe.wait_ge(part_ready, EXPERTS * c + e - 1)
                            for m in range(2):
                                mm = pe.matmul(out_ps[e % 2][:, m, :CT], proj[:, e, t, m * HC:(m + 1) * HC],
                                               hid[(i - LAG) % NHID][:], start=t == 0, stop=t == HT - 1)
                            mm.then_inc(tile_used, 1)

                run(pe, chunk)

            @block.scalar
            def _(act):
                def chunk(c):
                    for i in range(TILES):
                        e, t = divmod(i, HT)
                        if t == 0:
                            act.wait_ge(gate_spread, EXPERTS * c + e + 1)
                            if not (first(c) and e < 2):
                                act.wait_ge(part_ready, EXPERTS * c + e - 1)
                            act.activation(gate[e % 2][:], gate_ps[:, :CT], ACT.Copy).then_inc(gate_ready, 1)
                        act.wait_ge(hid_summed, TILES * c + i + 1)
                        if not (first(c) and i < NHID):
                            act.wait_ge(tile_used, TILES * c + i + 1 - NHID)
                        act.activation(hid[i % NHID][:], hid_ps[i % 3][:, :CT], ACT.Gelu_apprx_tanh
                                       ).then_inc(hid_ready, 1)

                run(act, chunk)

            @block.vector
            def _(dve):
                def chunk(c):
                    for e in range(EXPERTS):
                        dve.wait_ge(tile_used, TILES * c + HT * (e + 1))
                        dve.wait_ge(gate_ready, EXPERTS * c + e + 1)
                        if not (first(c) and e == 0):
                            dve.wait_ge(part_added, EXPERTS * c + e)
                        dve.tensor_tensor(part[e % 2][:], out_ps[e % 2][:, :, :CT],
                                          gate[e % 2][:, None, :].to_broadcast([HC, 2, CT]), ALU.mult
                                          ).then_inc(part_ready, 1)
                        dve.wait_ge(part_ready, EXPERTS * c + e + 1)
                        tokens = H[:, :, bass.ds(c * CT, CT)]
                        dve.tensor_tensor(tokens, tokens, part[e % 2][:], ALU.add).then_inc(part_added, 1)

                run(dve, chunk)


def quantised_ffn(nc, const, w1_d, w1t_d, b1_d, w2_d, b2_d, XN, H, out_d):
    with ExitStack() as ctx:
        def sb(what, shape, dt=F32):
            return ctx.enter_context(nc.sbuf_tensor(f"ffn_{what}", shape, dt))

        def sem(what):
            return nc.alloc_semaphore(f"ffn_{what}")

        w1 = sb("w1", [128, HT, C])
        w1t = sb("w1t", [HC, 2, HID])
        w2 = sb("w2", [HC, 2, HID])
        b1 = sb("b1", [128, HT])
        b2 = sb("b2", [HC, 2])
        w1q = sb("w1q", [HC, 2 * HID], BF16)
        w2q = sb("w2q", [128, HT * C], BF16)
        xr = [sb(f"xr{i}", [HC, 2, CT]) for i in range(2)]
        xq = [sb(f"xq{i}", [HC, 2, CT], BF16) for i in range(2)]
        hid = sb("hid", [128, HT, T])
        hr = [sb(f"hr{i}", [128, HT, CT]) for i in range(2)]
        hq = [sb(f"hq{i}", [128, HT, CT], BF16) for i in range(2)]
        cmax, cmin, cabs, wmax, ratio, root = (sb(w, [HC, 2]) for w in
                                               ("cmax", "cmin", "cabs", "wmax", "ratio", "root"))
        power, up, cs, ics, xscale = (sb(w, [HC, 2]) for w in ("power", "up", "cs", "ics", "xscale"))
        xs = sb("xs", [HC, 2, 2])
        ends, ends_all = sb("ends", [128, 2]), sb("ends_all", [128, 2])
        s1, inv1, s1x = sb("s1", [128, HT]), sb("inv1", [128, HT]), sb("s1x", [128, HT])
        s2, inv2, s2h = sb("s2", [HC, 2]), sb("inv2", [HC, 2]), sb("s2h", [HC, 2])
        habs, hmax, hall = sb("habs", [128, CHUNKS, HT]), sb("hmax", [128, 1]), sb("hall", [128, 1])
        step_h, inv_h = sb("step_h", [128, 1]), sb("inv_h", [128, 1])
        step_x, inv_x, low_x, top_x = (sb(w, [128, 1]) for w in ("step_x", "inv_x", "low_x", "top_x"))
        step_o, inv_o, low_o, top_o = (sb(w, [128, 1]) for w in ("step_o", "inv_o", "low_o", "top_o"))
        total = sb("total", [128, 1])
        omax, omin = sb("omax", [HC, 2, CHUNKS]), sb("omin", [HC, 2, CHUNKS])
        ps = [ctx.enter_context(nc.psum_tensor(f"ffn_ps{i}", [128, 512], F32)) for i in range(8)]
        O = XN

        def chained(dve, sem_):
            done = [0]

            def then(ins):
                ins.then_inc(sem_, 1)
                done[0] += 1
                dve.wait_ge(sem_, done[0])
            return then

        def asymmetric(dve, then, hi_lo, step, inv, low, top):
            then(dve.tensor_tensor(total[:], hi_lo[:, 0:1], hi_lo[:, 1:2], ALU.add))
            then(dve.tensor_scalar(step[:], total[:], 1.0 / 255.0, 1e-8, ALU.mult, ALU.max))
            then(dve.reciprocal(inv[:], step[:]))
            then(dve.tensor_tensor(total[:], hi_lo[:, 1:2], inv[:], ALU.mult))
            then(dve.tensor_scalar(total[:], total[:], ROUND, None, ALU.add))
            then(dve.tensor_scalar(low[:], total[:], ROUND, -1.0, ALU.subtract, ALU.mult))
            then(dve.tensor_scalar(top[:], low[:], 255.0, None, ALU.add))

        loaded, gathered, root_ready, ends_ready = map(sem, ("loaded", "gathered", "root_ready", "ends_ready"))
        chain_a, cs_ready, row_spread, ratio_ready = map(sem, ("chain_a", "cs_ready", "row_spread", "ratio_ready"))
        w1_ready, w2_ready, w1_turned, w2_turned, w_copied = map(
            sem, ("w1_ready", "w2_ready", "w1_turned", "w2_turned", "w_copied"))
        with nc.Block() as block:
            @block.sync
            def _(sp):
                for dst, d in ((w1, w1_d), (w1t, w1t_d), (b1, b1_d), (w2, w2_d), (b2, b2_d)):
                    sp.dma_start(dst[:], d).then_inc(loaded, 16)

            @block.gpsimd
            def _(pool):
                pool.wait_ge(ends_ready, 1)
                pool.partition_all_reduce(ends_all[:], ends[:], 128, RMAX).then_inc(gathered, 1)

            @block.scalar
            def _(act):
                act.wait_ge(ratio_ready, 1)
                act.activation(root[:], ratio[:], ACT.Sqrt).then_inc(root_ready, 1)
                for i in range(3):
                    act.wait_ge(w1_turned, i + 1)
                    act.activation(w1q[:, i * 512:(i + 1) * 512], ps[1 + i][:HC, :], ACT.Copy).then_inc(w_copied, 1)
                for i in range(3):
                    act.wait_ge(w2_turned, i + 1)
                    act.activation(w2q[:, i * 384:(i + 1) * 384], ps[4 + i][:, :384], ACT.Copy).then_inc(w_copied, 1)

            @block.tensor
            def _(pe):
                pe.wait_ge(cs_ready, 1)
                for half in range(2):
                    mm = pe.matmul(ps[0][:, half * HC:(half + 1) * HC],
                                   cs[:, half:half + 1].to_broadcast([HC, 128]), const["ident"][:HC, :HC],
                                   start=True, stop=True)
                mm.then_inc(row_spread, 1)
                pe.wait_ge(w1_ready, 1)
                for q in range(2 * HT):
                    half, t = divmod(q, HT)
                    mm = pe.transpose(ps[1 + q // 4][:HC, q % 4 * 128:(q % 4 + 1) * 128],
                                      w1[:, t, half * HC:(half + 1) * HC], const["ident"][:])
                    if q % 4 == 3:
                        mm.then_inc(w1_turned, 1)
                pe.wait_ge(w2_ready, 1)
                for q in range(2 * HT):
                    t, half = divmod(q, 2)
                    mm = pe.transpose(ps[4 + q // 4][:, q % 4 * HC:(q % 4 + 1) * HC],
                                      w2[:, half, t * 128:(t + 1) * 128], const["ident"][:HC, :HC])
                    if q % 4 == 3:
                        mm.then_inc(w2_turned, 1)

            @block.vector
            def _(dve):
                then = chained(dve, chain_a)

                def weight(w, s, inv, rows):
                    then(dve.tensor_reduce(s[:], w[:], AX.X, ALU.max, apply_absolute_value=True))
                    then(dve.tensor_scalar(s[:], s[:], 1.0 / 127.0, 1e-8, ALU.mult, ALU.max))
                    then(dve.reciprocal(inv[:], s[:]))
                    for r in range(rows):
                        last = dve.tensor_scalar(w[:, r, :], w[:, r, :], inv[:, r:r + 1], ROUND, ALU.mult, ALU.add)
                    then(last)
                    then(dve.tensor_scalar(w[:], w[:], ROUND, -128.0, ALU.subtract, ALU.max))

                then(dve.memset(ends[:], 0.0))
                then(dve.tensor_reduce(cmax[:], XN[:], AX.X, ALU.max))
                then(dve.tensor_reduce(cmin[:], XN[:], AX.X, ALU.min))
                then(dve.scalar_tensor_tensor(cabs[:], cmin[:], -1.0, cmax[:], ALU.mult, ALU.max))
                dve.wait_ge(loaded, 80)
                then(dve.tensor_reduce(wmax[:], w1t[:], AX.X, ALU.max, apply_absolute_value=True))
                then(dve.reciprocal(ratio[:], wmax[:]))
                then(dve.tensor_tensor(ratio[:], ratio[:], cabs[:], ALU.mult))
                dve.memset(total[:], 0.0).then_inc(ratio_ready, 1)
                dve.wait_ge(root_ready, 1)
                then(dve.tensor_scalar(power[:].bitcast(I32), root[:].bitcast(I32), 0x7F800000, None,
                                       ALU.bitwise_and))
                then(dve.scalar_tensor_tensor(up[:], power[:], 1.5, root[:], ALU.mult, ALU.is_lt))
                then(dve.tensor_tensor(up[:], power[:], up[:], ALU.mult))
                then(dve.tensor_tensor(cs[:], power[:], up[:], ALU.add))
                dve.reciprocal(ics[:], cs[:]).then_inc(cs_ready, 1)
                dve.wait_ge(cs_ready, 1)
                then(dve.tensor_tensor(xs[:, 0, :], cmax[:], ics[:], ALU.mult))
                then(dve.scalar_tensor_tensor(xs[:, 1, :], cmin[:], -1.0, ics[:], ALU.mult, ALU.mult))
                then(dve.tensor_reduce(ends[:HC, :], xs[:], AX.X, ALU.max))
                dve.tensor_scalar(ends[:], ends[:], 0.0, None, ALU.max).then_inc(ends_ready, 1)
                dve.wait_ge(row_spread, 1)
                then(dve.tensor_tensor(w1[:], w1[:], ps[0][:, None, :C].to_broadcast([128, HT, C]), ALU.mult))
                weight(w1, s1, inv1, HT)
                dve.tensor_scalar(w1[:], w1[:], 127.0, None, ALU.min).then_inc(w1_ready, 1)
                weight(w2, s2, inv2, 2)
                dve.tensor_scalar(w2[:], w2[:], 127.0, None, ALU.min).then_inc(w2_ready, 1)
                dve.wait_ge(gathered, 1)
                asymmetric(dve, then, ends_all, step_x, inv_x, low_x, top_x)
                then(dve.tensor_scalar(xscale[:], ics[:], inv_x[:HC, :], None, ALU.mult))
                then(dve.tensor_scalar(s1x[:], s1[:], step_x[:], None, ALU.mult))

        x_steps, xq_ready, hid_summed, hid_ready, hid_maxed = map(
            sem, ("x_steps", "xq_ready", "hid_summed", "hid_ready", "hid_maxed"))
        with nc.Block() as block:
            @block.vector
            def _(dve):
                def quantise(c):
                    tok = slice(c * CT, (c + 1) * CT)
                    x, b = xr[c % 2], c % 2
                    if c >= 1:
                        dve.wait_ge(x_steps, 3 * c)
                        dve.wait_ge(xq_ready, c)
                    if c >= 2:
                        dve.wait_ge(hid_summed, HT * (c - 1))
                    for half in range(2):
                        dve.tensor_scalar(x[:, half, :], XN[:, half, tok], xscale[:, half:half + 1], ROUND,
                                          ALU.mult, ALU.add).then_inc(x_steps, 1)
                    dve.wait_ge(x_steps, 3 * c + 2)
                    dve.tensor_scalar(x[:], x[:], ROUND, low_x[:HC, :], ALU.subtract, ALU.max).then_inc(x_steps, 1)
                    dve.wait_ge(x_steps, 3 * c + 3)
                    dve.tensor_scalar(xq[b][:], x[:], top_x[:HC, :], None, ALU.min).then_inc(xq_ready, 1)

                for c in range(CHUNKS + 1):
                    if c < CHUNKS:
                        quantise(c)
                    if c >= 1:
                        dve.wait_ge(hid_ready, HT * c)
                        dve.tensor_reduce(habs[:, c - 1, :], hid[:, :, (c - 1) * CT:c * CT], AX.X, ALU.max,
                                          apply_absolute_value=True).then_inc(hid_maxed, 1)

            @block.tensor
            def _(pe):
                for c in range(CHUNKS):
                    pe.wait_ge(xq_ready, c + 1)
                    for t in range(HT):
                        i = HT * c + t
                        if i >= 8:
                            pe.wait_ge(hid_ready, i - 7)
                        for half in range(2):
                            mm = pe.matmul(ps[i % 8][:, :CT], w1q[:, half * HID + t * 128:half * HID + (t + 1) * 128],
                                           xq[c % 2][:, half, :], start=half == 0, stop=half == 1)
                        mm.then_inc(hid_summed, 1)

            @block.scalar
            def _(act):
                for i in range(HT * CHUNKS):
                    c, t = divmod(i, HT)
                    act.wait_ge(hid_summed, i + 1)
                    act.activation(hid[:, t, c * CT:(c + 1) * CT], ps[i % 8][:, :CT], ACT.Gelu,
                                   scale=s1x[:, t:t + 1], bias=b1[:, t:t + 1]).then_inc(hid_ready, 1)

        chain_c, hmax_ready, hall_ready, scale_ready = map(sem, ("chain_c", "hmax_ready", "hall_ready", "scale_ready"))
        h_scaled, h_clipped, hq_ready, out_summed, out_ready, out_ranged = map(
            sem, ("h_scaled", "h_clipped", "hq_ready", "out_summed", "out_ready", "out_ranged"))
        with nc.Block() as block:
            @block.gpsimd
            def _(pool):
                pool.wait_ge(hmax_ready, 1)
                pool.partition_all_reduce(hall[:], hmax[:], 128, RMAX).then_inc(hall_ready, 1)

            @block.vector
            def _(dve):
                then = chained(dve, chain_c)
                dve.tensor_reduce(hmax[:], habs[:].rearrange("p a b -> p (a b)"), AX.X, ALU.max
                                  ).then_inc(hmax_ready, 1)
                dve.wait_ge(hall_ready, 1)
                then(dve.tensor_scalar(step_h[:], hall[:], 1.0 / 127.0, 1e-8, ALU.mult, ALU.max))
                then(dve.reciprocal(inv_h[:], step_h[:]))
                dve.tensor_scalar(s2h[:], s2[:], step_h[:HC, :], None, ALU.mult).then_inc(scale_ready, 1)
                for c in range(CHUNKS + 1):
                    if c < CHUNKS:
                        b = c % 2
                        dve.wait_ge(h_scaled, c + 1)
                        dve.tensor_scalar(hr[b][:], hr[b][:], ROUND, -128.0, ALU.subtract, ALU.max
                                          ).then_inc(h_clipped, 1)
                        dve.wait_ge(h_clipped, c + 1)
                        if c >= 2:
                            dve.wait_ge(out_summed, 2 * (c - 1))
                        dve.tensor_scalar(hq[b][:], hr[b][:], 127.0, None, ALU.min).then_inc(hq_ready, 1)
                    if c >= 1:
                        got = O[:, :, (c - 1) * CT:c * CT]
                        dve.wait_ge(out_ready, 2 * c)
                        dve.tensor_reduce(omax[:, :, c - 1], got, AX.X, ALU.max).then_inc(out_ranged, 1)
                        dve.tensor_reduce(omin[:, :, c - 1], got, AX.X, ALU.min).then_inc(out_ranged, 1)

            @block.scalar
            def _(act):
                act.wait_ge(scale_ready, 1)
                for c in range(CHUNKS + 1):
                    if c < CHUNKS:
                        if c >= 2:
                            act.wait_ge(hq_ready, c - 1)
                        act.activation(hr[c % 2][:], hid[:, :, c * CT:(c + 1) * CT], ACT.Identity,
                                       scale=inv_h[:], bias=ROUND).then_inc(h_scaled, 1)
                    if c >= 1:
                        for m in range(2):
                            i = 2 * (c - 1) + m
                            act.wait_ge(out_summed, i + 1)
                            act.activation(O[:, m, (c - 1) * CT:c * CT], ps[i % 8][:HC, :CT], ACT.Identity,
                                           scale=s2h[:, m:m + 1], bias=b2[:, m:m + 1]).then_inc(out_ready, 1)

            @block.tensor
            def _(pe):
                for c in range(CHUNKS):
                    pe.wait_ge(hq_ready, c + 1)
                    for m in range(2):
                        i = 2 * c + m
                        if i >= 8:
                            pe.wait_ge(out_ready, i - 7)
                        for t in range(HT):
                            mm = pe.matmul(ps[i % 8][:HC, :CT], w2q[:, t * C + m * HC:t * C + (m + 1) * HC],
                                           hq[c % 2][:, t, :], start=t == 0, stop=t == HT - 1)
                        mm.then_inc(out_summed, 1)

        chain_d, oends_ready, oall_ready, o_steps, o_ready, h_ready, stored = map(
            sem, ("chain_d", "oends_ready", "oall_ready", "o_steps", "o_ready", "h_ready", "stored"))
        with nc.Block() as block:
            @block.vector
            def _(dve):
                then = chained(dve, chain_d)
                then(dve.memset(ends[:], 0.0))
                then(dve.tensor_reduce(cmax[:], omax[:], AX.X, ALU.max))
                then(dve.tensor_reduce(cmin[:], omin[:], AX.X, ALU.min))
                then(dve.tensor_copy(xs[:, 0, :], cmax[:]))
                then(dve.tensor_scalar(xs[:, 1, :], cmin[:], -1.0, None, ALU.mult))
                then(dve.tensor_reduce(ends[:HC, :], xs[:], AX.X, ALU.max))
                dve.tensor_scalar(ends[:], ends[:], 0.0, None, ALU.max).then_inc(oends_ready, 1)
                dve.wait_ge(oall_ready, 1)
                asymmetric(dve, then, ends_all, step_o, inv_o, low_o, top_o)
                for c in range(CHUNKS):
                    o = O[:, :, c * CT:(c + 1) * CT]
                    dve.tensor_scalar(o, o, inv_o[:HC, :], ROUND, ALU.mult, ALU.add).then_inc(o_steps, 1)
                    dve.wait_ge(o_steps, 2 * c + 1)
                    dve.tensor_scalar(o, o, ROUND, low_o[:HC, :], ALU.subtract, ALU.max).then_inc(o_steps, 1)
                    dve.wait_ge(o_steps, 2 * c + 2)
                    dve.tensor_scalar(o, o, top_o[:HC, :], step_o[:HC, :], ALU.min, ALU.mult).then_inc(o_ready, 1)

            @block.gpsimd
            def _(pool):
                pool.wait_ge(oends_ready, 1)
                pool.partition_all_reduce(ends_all[:], ends[:], 128, RMAX).then_inc(oall_ready, 1)
                for c in range(CHUNKS):
                    tok = slice(c * CT, (c + 1) * CT)
                    pool.wait_ge(o_ready, c + 1)
                    pool.tensor_tensor(H[:, :, tok], H[:, :, tok], O[:, :, tok], ALU.add).then_inc(h_ready, 1)

            @block.sync
            def _(sp):
                for c in range(CHUNKS):
                    sp.wait_ge(h_ready, c + 1)
                    sp.dma_start(out_d[:, :, c * CT:(c + 1) * CT], H[:, :, c * CT:(c + 1) * CT]).then_inc(stored, 16)
                sp.wait_ge(stored, 16 * CHUNKS)


def tower(nc, d, out):
    with ExitStack() as ctx:
        def sb(what, shape, dt=F32):
            return ctx.enter_context(nc.sbuf_tensor(what, shape, dt))

        const = {"ident": sb("ident", [128, 128]), "mean": sb("mean", [HC, HC]), "sel": sb("sel", [96, 32], BF16),
                 "ident_d": d["ident"]}
        H = sb("H", [HC, 2, T])
        XN = sb("XN", [HC, 2, T])

        embed(nc, const, d["patches"], d["w_tok"], H)
        ln_signals = norm_signals(nc, "ln")
        normalise(nc, const, "ln1", ln_signals, 0, H, XN, "layer")
        with nc.cleanup_on_exit(), ExitStack() as attn:
            Y = attn.enter_context(nc.sbuf_tensor("Y", [HC, 2, T], F32))
            gain = attn.enter_context(nc.sbuf_tensor("ln_gain", [HC, 2], F32))
            shift = attn.enter_context(nc.sbuf_tensor("ln_shift", [HC, 2], F32))
            w0 = {w: d[f"m0_{w}"] for w in ("par", "in_w", "xp_w", "dt_w", "out_w")}
            for i, direction in enumerate(("forward", "backward")):
                mamba(nc, const, direction, 1, w0, XN, Y, direction, {"w": d["bm_in_w"][i], "b": d["bm_in_b"][i]})
            project(nc, "bm_out", d["bm_out_w"], d["bm_out_b"], Y, XN, d["ln_g"], d["ln_b"], gain, shift)
            normalise(nc, const, "ln_attn", norm_signals(nc, "ln_attn"), 0, Y, H, "layer_add", gain, shift)
        normalise(nc, const, "ln2", ln_signals, 1 * CHUNKS, H, XN, "layer")
        with nc.cleanup_on_exit(), ExitStack() as moe:
            gates = moe.enter_context(nc.sbuf_tensor("gates", [EXPERTS, T], F32))
            route(nc, const, d["w_gate"], d["lower"], XN, gates)
            experts(nc, const, d["w_fc"], d["w_proj"], XN, gates, H)
        normalise(nc, const, "ln3", ln_signals, 2 * CHUNKS, H, XN, "layer")
        w1 = {w: d[f"m1_{w}"] for w in ("par", "in_w", "xp_w", "dt_w", "out_w")}
        mamba(nc, const, "inner", LAYERS, w1, XN, XN)
        with ExitStack() as fin:
            gain = fin.enter_context(nc.sbuf_tensor("final_gain", [HC, 2], F32))
            gain_loaded = nc.alloc_semaphore("gain_loaded")
            with nc.Block() as block:
                @block.sync
                def _(sp):
                    sp.dma_start(gain[:], d["final_norm"]).then_inc(gain_loaded, 16)
                    sp.wait_ge(gain_loaded, 16)
            normalise(nc, const, "rms_final", norm_signals(nc, "rms_final"), 0, XN, H, "rms_add", gain)
        normalise(nc, const, "ln4", ln_signals, 3 * CHUNKS, H, XN, "layer")
        quantised_ffn(nc, const, d["w1"], d["w1t"], d["b1"], d["w2"], d["b2"], XN, H, out)


def _layout(np, a):
    def halves(v):
        return v.reshape(2, HC, *v.shape[1:]).swapaxes(0, 1)

    def tiles(v):
        return v.reshape(-1, 128, *v.shape[1:]).swapaxes(0, 1)

    d = {}
    x = a["x"].reshape(SEQS, 3, 7, 16, 7, 16).transpose(1, 3, 5, 0, 2, 4).reshape(768, T)
    d["patches"] = tiles(x).reshape(128, PK, CHUNKS, CT).transpose(2, 0, 1, 3)
    d["w_tok"] = tiles(a["L0_tok_W"].T)
    bm = a["L0_attn_bm_in_w"].T.reshape(C, 2, C)
    d["bm_in_w"] = np.stack([halves(bm[:, i]) for i in range(2)])
    d["bm_in_b"] = np.stack([halves(b) for b in a["L0_attn_bm_in_b"].reshape(2, C)])
    d["bm_out_w"], d["bm_out_b"] = halves(a["L0_attn_bm_out_w"].T), halves(a["L0_attn_bm_out_b"])
    d["ln_g"], d["ln_b"] = halves(a["L0_attn_ln_g"]), halves(a["L0_attn_ln_b"])

    def block(in_w, conv_w, conv_b, xp_w, dt_w, dt_b, a_log, dp, out_w, norm_w):
        n, r = len(in_w), dt_w.shape[-1]
        par = np.zeros((128, n, P_END), np.float32)
        for i in range(n):
            par[:, i, P_A:P_D] = tiles(a_log[i]).reshape(128, -1)
            par[:, i, P_D:P_CW] = tiles(dp[i])
            par[:, i, P_CW:P_CB] = tiles(conv_w[i]).reshape(128, -1)
            par[:, i, P_CB:P_DTB] = tiles(conv_b[i])
            par[:, i, P_DTB:P_NW] = tiles(dt_b[i])
            if norm_w is not None:
                par[:HC, i, P_NW:] = halves(norm_w[i])
        dt_rows = np.zeros((n, RANK, DT * 128), np.float32)
        dt_rows[:, :r] = dt_w.transpose(0, 2, 1)
        xp = np.zeros((n, LOW, DT * 128), np.float32)
        xp[:, :2 * NS] = xp_w[:, r:]
        xp[:, 64:64 + r] = xp_w[:, :r]
        return {
            "par": par, "dt_w": dt_rows,
            "in_w": np.stack([halves(w.T) for w in in_w]),
            "xp_w": np.stack([tiles(w.T).reshape(128, -1) for w in xp]),
            "out_w": np.stack([tiles(w.T).reshape(128, -1) for w in out_w]),
        }

    names = ("in_w", "conv_w", "conv_b", "xproj_w", "dt_w", "dt_b", "A_log", "D", "out_w")
    m0 = block(*(a[f"L0_attn_m_{n}"][None] for n in names), None)
    names = ("in_proj_w", "conv_w", "conv_b", "x_proj_w", "dt_proj_w", "dt_proj_b", "A_log", "D", "out_proj_w",
             "norm_w")
    m1 = block(*(a[f"L1_attn_{n}"] for n in names))
    d.update({f"m0_{k}": v for k, v in m0.items()})
    d.update({f"m1_{k}": v for k, v in m1.items()})
    d["w_gate"] = halves(a["L0_ffn_w_gate"])
    d["w_fc"] = halves(a["L0_ffn_w_fc"].reshape(C, HID, EXPERTS)).transpose(0, 3, 1, 2)
    d["w_proj"] = tiles(a["L0_ffn_w_proj"].reshape(HID, C, EXPERTS)).transpose(0, 3, 1, 2)
    d["final_norm"] = halves(a["L1_attn_final_norm_w"])
    d["w1"], d["w1t"], d["b1"] = tiles(a["L1_ffn_w1"]), halves(a["L1_ffn_w1"].T), tiles(a["L1_ffn_b1"])
    d["w2"], d["b2"] = halves(a["L1_ffn_w2"]), halves(a["L1_ffn_b2"])
    d["ident"] = np.eye(128, dtype=np.float32)
    d["lower"] = np.broadcast_to(np.tri(EXPERTS, k=-1, dtype=np.float32).reshape(1, -1), (128, EXPERTS ** 2))
    return {k: np.ascontiguousarray(v) for k, v in d.items()}


def kernel(**inputs):
    import numpy as np
    import concourse.bacc as bacc
    from concourse.bass_utils import run_bass_kernel_spmd

    nc = bacc.Bacc("TRN2", target_bir_lowering=False, num_devices=1)
    laid = _layout(np, {k: np.asarray(v) for k, v in inputs.items()})
    aps = {k: nc.dram_tensor(f"in_{k}", v.shape, mybir.dt.from_np(v.dtype), kind="ExternalInput").ap()
           for k, v in laid.items()}
    out = nc.dram_tensor("out", (HC, 2, T), F32, kind="ExternalOutput").ap()
    tower(nc, aps, out)
    r = run_bass_kernel_spmd(nc, [{f"in_{k}": v for k, v in laid.items()}], core_ids=[0])
    got = r.results[0]["out"]
    return np.ascontiguousarray(got.transpose(2, 1, 0).reshape(SEQS, LEN, C))
```
